# Optimizing a Trainium2 kernel written in Bass

```python
import numpy as np
import jax
import jax.numpy as jnp

def _softmax(x, axis=-1):
    return jax.nn.softmax(x, axis=axis)

def _gelu(x):
    return jax.nn.gelu(x, approximate=True)

def _silu(x):
    return jax.nn.silu(x)

def _sigmoid(x):
    return jax.nn.sigmoid(x)

def _layernorm(x, axis=-1, eps=1e-05):
    m = jnp.mean(x, axis=axis, keepdims=True)
    v = jnp.var(x, axis=axis, keepdims=True)
    return (x - m) / jnp.sqrt(v + eps)

def _scatter_add(tgt, idx, src, axis=0):
    return tgt.at[idx].add(src)

def _segment_sum(src, seg, n):
    return jax.ops.segment_sum(src, seg, n)
kernel_name = 'mk_decoder_preln_d1_seqx_r2_2b562a'

def setup_inputs(seed: int=0):
    np.random.seed(seed)
    _w = jnp.asarray

    def _rec_inputs():
        import jax
        import jax.numpy as jnp
        _rk = jax.random.key(seed)
        x = -0.0002928 + 1 * jax.random.normal(jax.random.fold_in(_rk, 1), (2, 2048, 512), jnp.float32)
        _lenS = 2048 - jax.random.randint(jax.random.fold_in(_rk, 7), (2,), 0, max(1, 2048 // 4) + 1, jnp.int32)
        _lenS2 = 128 - jax.random.randint(jax.random.fold_in(_rk, 8), (2,), 0, max(1, 128 // 4) + 1, jnp.int32)
        _ctx_1024P = jax.random.normal(jax.random.fold_in(_rk, 11), (2, 16, 512), jnp.float32)
        _ctx_1024c = jax.random.dirichlet(jax.random.fold_in(_rk, 511), 0.3 * jnp.ones((16,), jnp.float32), (2, 128))
        _ctx_1024t = jnp.einsum('bsk,bkd->bsd', _ctx_1024c, _ctx_1024P)
        _ctx_1024t = _ctx_1024t * jax.lax.rsqrt(jnp.mean(jnp.square(_ctx_1024t)) + 1e-12) * 0.953939
        ctx_1024 = -1.39393e-06 + 0.999914 * (_ctx_1024t + 0.3 * jax.random.normal(jax.random.fold_in(_rk, 611), (2, 128, 512), jnp.float32))
        _validS = jnp.arange(2048)[None, :] < _lenS[:, None]
        _validS2 = jnp.arange(128)[None, :] < _lenS2[:, None]
        _causal = jnp.tril(jnp.ones((2048, 2048), dtype=bool))
        mask_SxS2_bk0 = jnp.logical_not(jnp.broadcast_to(_validS2[0:1, :], (2048, 128)))
        return (x, ctx_1024, mask_SxS2_bk0)
    x, ctx_1024, mask_SxS2_bk0 = _rec_inputs()

    def _L0_attn_setup():
        import jax, jax.numpy as jnp
        import numpy as np
        B, T, C = (4, 1024, 512)
        QH = 4
        D = C // QH
        EPS = 1e-05

        def _layernorm(x, g, b):
            mu = jnp.mean(x, axis=-1, keepdims=True)
            var = jnp.mean(jnp.square(x - mu), axis=-1, keepdims=True)
            return (x - mu) * jax.lax.rsqrt(var + EPS) * g + b
        key = jax.random.key(seed)
        k1, k2, k3 = jax.random.split(key, 3)
        residual = jax.random.normal(k1, (B, T, C), dtype=jnp.float32)
        w_fc = jax.random.normal(k2, (C, C), dtype=jnp.float32) * (1.0 / np.sqrt(C))
        w_proj = jax.random.normal(k3, (C, C), dtype=jnp.float32) * (1.0 / np.sqrt(C))
        ln_g = jnp.ones((C,), dtype=jnp.float32)
        ln_b = jnp.zeros((C,), dtype=jnp.float32)
        return {'residual': residual, 'w_fc': w_fc, 'w_proj': w_proj, 'ln_g': ln_g, 'ln_b': ln_b}
    _L0_attn_all = _L0_attn_setup()
    _L0_attn_in = {k: v for k, v in _L0_attn_all.items() if k in ('w_fc', 'w_proj', 'ln_g', 'ln_b')}
    del _L0_attn_all

    def _L0_xattn_setup():
        import jax, jax.numpy as jnp
        import numpy as np
        H = 16
        DK = 64
        DV = 64
        DIM = 512

        def _split_heads(x, h):
            x = x.reshape(x.shape[:-1] + (h, -1))
            return jnp.swapaxes(x, -2, -3)

        def _merge_heads(x):
            x = jnp.swapaxes(x, -2, -3)
            return x.reshape(x.shape[:-2] + (-1,))
        key = jax.random.key(seed)
        ks = jax.random.split(key, 8)
        B, T = (2, 1024)
        q = jax.random.normal(ks[0], (B, T, DIM), dtype=jnp.float32)
        k = jax.random.normal(ks[1], (B, T, DIM), dtype=jnp.float32)
        v = jax.random.normal(ks[2], (B, T, DIM), dtype=jnp.float32)
        mask = jnp.tril(jnp.ones((T, T), dtype=bool))
        s = 1.0 / np.sqrt(DIM)
        Wq = jax.random.normal(ks[3], (DIM, H * DK), dtype=jnp.float32) * s
        Wk = jax.random.normal(ks[4], (DIM, H * DK), dtype=jnp.float32) * s
        Wv = jax.random.normal(ks[5], (DIM, H * DV), dtype=jnp.float32) * s
        Wo = jax.random.normal(ks[6], (H * DV, DIM), dtype=jnp.float32) * s
        return {'q': q, 'k': k, 'v': v, 'mask': mask, 'Wq': Wq, 'Wk': Wk, 'Wv': Wv, 'Wo': Wo}
    _L0_xattn_all = _L0_xattn_setup()
    _L0_xattn_in = {k: v for k, v in _L0_xattn_all.items() if k in ('Wq', 'Wk', 'Wv', 'Wo')}
    del _L0_xattn_all

    def _L0_ffn_setup():
        import jax, jax.numpy as jnp
        import numpy as np
        H = 512
        I = 1024
        E = 32
        B, S = (4, 1024)

        def _grouped_mm(a, w, group_sizes):
            return jax.lax.ragged_dot(a, w, group_sizes)

        def _swiglu(x, gw, uw, dw):
            return jax.nn.silu(x @ gw) * (x @ uw) @ dw
        key = jax.random.key(seed)
        ks = jax.random.split(key, 8)
        scale = 0.02
        inp = {'hidden_states': jax.random.normal(ks[0], (B, S, H), dtype=jnp.float32), 'gate_w': jax.random.normal(ks[1], (H, E), dtype=jnp.float32) * scale, 'shared_gate_w': jax.random.normal(ks[2], (H, I), dtype=jnp.float32) * scale, 'shared_up_w': jax.random.normal(ks[3], (H, I), dtype=jnp.float32) * scale, 'shared_down_w': jax.random.normal(ks[4], (I, H), dtype=jnp.float32) * scale, 'routed_gate_w': jax.random.normal(ks[5], (E, H, I), dtype=jnp.float32) * scale, 'routed_up_w': jax.random.normal(ks[6], (E, H, I), dtype=jnp.float32) * scale, 'routed_down_w': jax.random.normal(ks[7], (E, I, H), dtype=jnp.float32) * scale}
        return inp
    _L0_ffn_all = _L0_ffn_setup()
    _L0_ffn_in = {k: v for k, v in _L0_ffn_all.items() if k in ('gate_w', 'shared_gate_w', 'shared_up_w', 'shared_down_w', 'routed_gate_w', 'routed_up_w', 'routed_down_w')}
    del _L0_ffn_all
    return {'x': x, 'ctx_1024': ctx_1024, 'mask_SxS2_bk0': mask_SxS2_bk0, 'L0_attn_w_fc': _L0_attn_in['w_fc'], 'L0_attn_w_proj': _L0_attn_in['w_proj'], 'L0_attn_ln_g': _L0_attn_in['ln_g'], 'L0_attn_ln_b': _L0_attn_in['ln_b'], 'L0_xattn_Wq': _L0_xattn_in['Wq'], 'L0_xattn_Wk': _L0_xattn_in['Wk'], 'L0_xattn_Wv': _L0_xattn_in['Wv'], 'L0_xattn_Wo': _L0_xattn_in['Wo'], 'L0_ffn_gate_w': _L0_ffn_in['gate_w'], 'L0_ffn_shared_gate_w': _L0_ffn_in['shared_gate_w'], 'L0_ffn_shared_up_w': _L0_ffn_in['shared_up_w'], 'L0_ffn_shared_down_w': _L0_ffn_in['shared_down_w'], 'L0_ffn_routed_gate_w': _L0_ffn_in['routed_gate_w'], 'L0_ffn_routed_up_w': _L0_ffn_in['routed_up_w'], 'L0_ffn_routed_down_w': _L0_ffn_in['routed_down_w']}

def reference(x, ctx_1024, mask_SxS2_bk0, L0_attn_w_fc, L0_attn_w_proj, L0_attn_ln_g, L0_attn_ln_b, L0_xattn_Wq, L0_xattn_Wk, L0_xattn_Wv, L0_xattn_Wo, L0_ffn_gate_w, L0_ffn_shared_gate_w, L0_ffn_shared_up_w, L0_ffn_shared_down_w, L0_ffn_routed_gate_w, L0_ffn_routed_up_w, L0_ffn_routed_down_w):
    import jax
    import jax.numpy as jnp

    def _L0_attn_ref(residual, w_fc, w_proj, ln_g, ln_b):
        import jax, jax.numpy as jnp
        import numpy as np
        B, T, C = (4, 1024, 512)
        QH = 4
        D = C // QH
        EPS = 1e-05

        def _layernorm(x, g, b):
            mu = jnp.mean(x, axis=-1, keepdims=True)
            var = jnp.mean(jnp.square(x - mu), axis=-1, keepdims=True)
            return (x - mu) * jax.lax.rsqrt(var + EPS) * g + b
        Bx, Tx, Cx = residual.shape
        x = _layernorm(residual, ln_g, ln_b)
        q = x.reshape(Bx, Tx, QH, D).transpose(0, 2, 1, 3)
        k = w_fc.reshape(-1, D)
        v = w_proj.T.reshape(-1, D)
        scores = jnp.einsum('bhtd,sd->bhts', q, k)
        p = jnp.square(jax.nn.relu(scores))
        out = jnp.einsum('bhts,sd->bhtd', p, v)
        out = out.transpose(0, 2, 1, 3).reshape(Bx, Tx, Cx)
        return residual + out

    def _L0_xattn_ref(q, k, v, mask, Wq, Wk, Wv, Wo):
        import jax, jax.numpy as jnp
        import numpy as np
        H = 16
        DK = 64
        DV = 64
        DIM = 512

        def _split_heads(x, h):
            x = x.reshape(x.shape[:-1] + (h, -1))
            return jnp.swapaxes(x, -2, -3)

        def _merge_heads(x):
            x = jnp.swapaxes(x, -2, -3)
            return x.reshape(x.shape[:-2] + (-1,))
        q_i = _split_heads(q @ Wq, H)
        k_i = _split_heads(k @ Wk, H)
        v_i = _split_heads(v @ Wv, H)
        s_qk = jnp.einsum('...hik,...hjk->...hij', q_i, k_i) / jnp.sqrt(jnp.asarray(DK, dtype=q_i.dtype))
        neg = -jnp.finfo(s_qk.dtype).max
        s_qk = jnp.where(mask, s_qk, neg)
        attn = jax.nn.softmax(s_qk, axis=-1)
        vals = jnp.einsum('...hij,...hjv->...hiv', attn, v_i)
        return _merge_heads(vals) @ Wo

    def _L0_ffn_ref(hidden_states, gate_w, shared_gate_w, shared_up_w, shared_down_w, routed_gate_w, routed_up_w, routed_down_w):
        import jax, jax.numpy as jnp
        import numpy as np
        H = 512
        I = 1024
        E = 32
        B, S = (4, 1024)

        def _grouped_mm(a, w, group_sizes):
            return jax.lax.ragged_dot(a, w, group_sizes)

        def _swiglu(x, gw, uw, dw):
            return jax.nn.silu(x @ gw) * (x @ uw) @ dw
        b, s, h = hidden_states.shape
        x = hidden_states.reshape(-1, h)
        shared_out = _swiglu(x, shared_gate_w, shared_up_w, shared_down_w)
        logits = x @ gate_w
        topk_ids = jnp.argmax(logits, axis=-1)
        topk_val = jnp.max(logits, axis=-1)
        scores = jax.nn.sigmoid(topk_val)[:, None]
        xs = x * scores
        tokens_per_expert = jnp.zeros((E,), jnp.int32).at[topk_ids].add(1)
        order = jnp.argsort(topk_ids)
        sorted_x = xs[order]
        g = _grouped_mm(sorted_x, routed_gate_w, tokens_per_expert)
        u = _grouped_mm(sorted_x, routed_up_w, tokens_per_expert)
        d = _grouped_mm(jax.nn.silu(g) * u, routed_down_w, tokens_per_expert)
        inv = jnp.argsort(order)
        routed_out = d[inv]
        return (shared_out + routed_out).reshape(b, s, h)
    x = x + _L0_attn_ref(_layernorm(x, axis=-1), L0_attn_w_fc, L0_attn_w_proj, L0_attn_ln_g, L0_attn_ln_b)
    x = x + _L0_xattn_ref(_layernorm(x, axis=-1), ctx_1024, ctx_1024, mask_SxS2_bk0, L0_xattn_Wq, L0_xattn_Wk, L0_xattn_Wv, L0_xattn_Wo)
    x = x + _L0_ffn_ref(_layernorm(x, axis=-1), L0_ffn_gate_w, L0_ffn_shared_gate_w, L0_ffn_shared_up_w, L0_ffn_shared_down_w, L0_ffn_routed_gate_w, L0_ffn_routed_up_w, L0_ffn_routed_down_w)
    return x

_drawn_inputs = setup_inputs


def setup_inputs(seed=0):
    import zlib

    import numpy as np

    out = dict(_drawn_inputs(seed))
    spreads = {'L0_attn_ln_g': (1.0, 0.2), 'L0_attn_ln_b': (0.0, 0.1)}
    factors = {'L0_ffn_gate_w': 3.802,
     'L0_ffn_routed_gate_w': 3.784,
     'L0_ffn_routed_up_w': 3.749,
     'L0_ffn_routed_down_w': 3.742,
     'L0_ffn_shared_gate_w': 3.907,
     'L0_ffn_shared_up_w': 3.801,
     'L0_ffn_shared_down_w': 3.805}
    for name, (base, spread) in spreads.items():
        noise = np.random.default_rng([zlib.crc32(name.encode()), seed]).standard_normal(out[name].shape)
        drawn = base * np.exp(spread * noise) if base else spread * noise
        out[name] = jnp.asarray(drawn.astype(out[name].dtype))
    for name, factor in factors.items():
        out[name] = (out[name] * factor).astype(out[name].dtype)
    return out
```

```python
from contextlib import ExitStack

import concourse.bass as bass
from concourse import mybir

TOK, C, P = 4096, 512, 128
NB = 2
KC = C // P
TILES = TOK // P
GT = 4
GTOK = GT * P
GROUPS = TOK // GTOK
EPS = 1e-5


class Link:

    def __init__(self, eng, sem, base=0):
        self.eng, self.sem, self.base, self.n = eng, sem, base, 0

    def __call__(self, ins):
        self.n += 1
        ins.then_inc(self.sem, 1)
        self.eng.wait_ge(self.sem, self.base + self.n)


def rsqrt(nc, link, y, t, v, ALU, I32):
    link(nc.vector.tensor_single_scalar(t.bitcast(I32), v.bitcast(I32), 1, op=ALU.logical_shift_right))
    link(nc.vector.tensor_scalar(y.bitcast(I32), t.bitcast(I32), -1.0, float(0x5F3759DF), ALU.mult, ALU.add))
    for _ in range(4):
        link(nc.vector.scalar_tensor_tensor(out=t, in0=y, scalar=-0.5, in1=y, op0=ALU.mult, op1=ALU.mult))
        link(nc.vector.tensor_tensor(t, t, v, ALU.mult))
        link(nc.vector.scalar_tensor_tensor(out=y, in0=t, scalar=1.5, in1=y, op0=ALU.add, op1=ALU.mult))


def split_matmuls(nc, out, a, b, first, last):
    nc.tensor.matmul(out, a[0], b[0], start=first, stop=False)
    nc.tensor.matmul(out, a[0], b[1], start=False, stop=False)
    return nc.tensor.matmul(out, a[1], b[0], start=False, stop=last)


def self_attention(nc, ident, stats, x, w_fc, w_proj, ln_g, ln_b, x1, mybir, bass, ExitStack):
    F32, F32R, I32 = mybir.dt.float32, mybir.dt.float32r, mybir.dt.int32
    ALU, ACT = mybir.AluOpType, mybir.ActivationFunctionType
    NH = C // P
    S = C * C // P
    SC = S // P
    NPAIR = SC // 2
    POOL_LOW = (1, 4, 6)
    NPL = len(POOL_LOW)
    x_t = x.rearrange("(t p) c -> p t c", p=P)
    x1_t = x1.rearrange("(t p) c -> p t c", p=P)
    with ExitStack() as ctx:
        sb = lambda n, s, d=F32: ctx.enter_context(nc.sbuf_tensor("a_" + n, s, d))
        ps = lambda n, s: ctx.enter_context(nc.psum_tensor("a_" + n, s, F32))
        sem = lambda n: ctx.enter_context(nc.semaphore("a_" + n))
        kH, kL = (sb(n, [P, SC, P], F32R) for n in ("kH", "kL"))
        vH, vL = (sb(n, [P, SC, P], F32R) for n in ("vH", "vL"))
        qH, qL = (sb(n, [P, 2, NH, GTOK], F32R) for n in ("qH", "qL"))
        base = sb("base", [P, 2, GT, C])
        gB, bB = sb("gB", [P, C]), sb("bB", [P, C])
        wf, wp = sb("wf", [P, KC, C]), sb("wp", [P, KC, C])
        xg = sb("xg", [P, 2, GT, C])
        st, mv = sb("st", [P, TILES, 6]), sb("mv", [P, TILES, 2])
        v1, v2, r1, r2, tmp = (sb(n, [P, TILES]) for n in ("v1", "v2", "r1", "r2", "tmp"))
        xb, y, qn = sb("xb", [P, 2, C]), sb("y", [P, C]), sb("qn", [P, C])
        r, p = sb("r", [P, 2, 2, GTOK]), sb("p", [P, 2, 2, GTOK])
        pH, pL = (sb(n, [P, 4, 2, GTOK], F32R) for n in ("pH", "pL"))
        oT, o1 = sb("oT", [P, GTOK]), sb("o1", [P, 2, GT, P])
        pS = [ps(f"pS{i}", [P, 2, GTOK]) for i in range(2)]
        pO = [ps(f"pO{i}", [P, GTOK]) for i in range(2)]
        pX, pT = ps("pX", [P, NH, P]), ps("pT", [P, GT, P])
        kv = [pS[i][:, 0, :] for i in range(2)]

        names = ("ident0 ident w_in gb_in stat_in0 stat_in1 stat own_dve own_pool kv_t kvH kvL x_in0 x_in1 prep affined based"
                 " xt qH qL score relu pH p lowD lowP pv oT ot o1 out0 out1").split()
        s = {n: sem(n) for n in names}

        def pools(k, c):
            return NPL * k + sum(1 for m in POOL_LOW if m <= c)

        def dves(k, c):
            return (NPAIR - NPL) * k + sum(1 for m in range(c + 1) if m not in POOL_LOW)

        def wait_low(eng, k, c):
            if c < 0:
                k, c = k - 1, c + NPAIR
            if c in POOL_LOW:
                eng.wait_ge(s["lowP"], pools(k, c))
            else:
                eng.wait_ge(s["lowD"], dves(k, c))

        def groups(eng, body):
            body(0, True, False)
            with eng.Fori(1, GROUPS - 1) as g:
                body(g, False, False)
            body(GROUPS - 1, False, True)

        block = ctx.enter_context(nc.Block())

        @block.sync
        def _(sp):
            sp.dma_start(wf[:, :, :], w_fc.rearrange("(a p) c -> p a c", p=P)).then_inc(s["w_in"], 16)
            sp.dma_start(wp[:, :, :], w_proj.rearrange("(a p) c -> p a c", p=P)).then_inc(s["w_in"], 16)
            for row, tile in ((ln_g, gB), (ln_b, bB)):
                sp.dma_start(tile[:, :], row.rearrange("(o c) -> o c", o=1).to_broadcast([P, C])).then_inc(s["gb_in"], 16)
            for g in range(GROUPS):
                if g >= 2:
                    sp.wait_ge(s["stat"], GT * (g - 1))
                sp.dma_start(xg[:, g % 2, :, :], x_t[:, g * GT:(g + 1) * GT, :]).then_inc(s[f"stat_in{g % 2}"], 16)

            def load(t, slot):
                sp.dma_start(xb[:, slot, :], x_t[:, bass.ds(t, 1), :].rearrange("p o c -> p (o c)")).then_inc(s[f"x_in{slot}"], 16)
            for t in range(GT):
                if t >= 2:
                    sp.wait_ge(s["based"], t - 1)
                load(t, t % 2)

            def body(g, first, last):
                for h in range(NH):
                    k = g * NH + h
                    if not last:
                        sp.wait_ge(s["based"], k + GT - 1)
                        load(k + GT, h % 2)
                    if not (first and h == 0):
                        sp.wait_ge(s["o1"], k)
                        store(g if h else g - 1, (h - 1) % NH)

            def store(g, h):
                sp.dma_start(x1_t[:, bass.ds(g * GT, GT), h * P:(h + 1) * P], o1[:, h % 2, :, :]).then_inc(s[f"out{h % 2}"], 16)
            groups(sp, body)
            sp.wait_ge(s["o1"], GROUPS * NH)
            store(GROUPS - 1, NH - 1)
            for slot in range(2):
                sp.wait_ge(s[f"out{slot}"], 16 * GROUPS * NH // 2)

        @block.gpsimd
        def _(pool):
            nc.gpsimd.memset(ident[:, :], 0.0).then_inc(s["ident0"], 1)
            pool.wait_ge(s["ident0"], 1)
            nc.gpsimd.affine_select(out=ident[:, :], in_=ident[:, :], compare_op=ALU.not_equal, fill=1.0,
                                    base=0, pattern=[[-1, P]], channel_multiplier=1).then_inc(s["ident"], 1)
            pool.wait_ge(s["gb_in"], 32)

            def affine(t, link):
                pool.wait_ge(s["prep"], 2 * t + 2)
                link(nc.gpsimd.tensor_tensor(qn[:, :], qn[:, :], gB[:, :], ALU.mult))
                nc.gpsimd.tensor_tensor(qn[:, :], qn[:, :], bB[:, :], ALU.add).then_inc(s["affined"], 1)

            def add_base(g, t, h):
                nc.gpsimd.tensor_tensor(base[:, bass.ds(g % 2, 1), h, :].rearrange("p o c -> p (o c)"),
                                        xb[:, h % 2, :], y[:, :], ALU.add).then_inc(s["based"], 1)

            def low(k, c):
                pool.wait_ge(s["pH"], NPAIR * k + c + 1)
                pool.wait_ge(s["p"], NPAIR * k + c + 1)
                nc.gpsimd.tensor_tensor(pL[:, c % 4, :, :], p[:, c % 2, :, :], pH[:, c % 4, :, :].bitcast(F32),
                                        ALU.subtract).then_inc(s["lowP"], 1)
            for t in range(GT):
                affine(t, Link(pool, s["own_pool"], t))
                add_base(0, t, t)

            def body(g, first, last):
                for h in range(NH):
                    k = g * NH + h
                    low(k, 1)
                    if not last:
                        affine(k + GT, Link(pool, s["own_pool"], k + GT))
                    low(k, 4)
                    if not last:
                        if not first:
                            pool.wait_ge(s["o1"], g * NH)
                        add_base(g + 1, k + GT, h)
                    low(k, 6)
            groups(pool, body)

        @block.scalar
        def _(act):
            def high(out, in_, func=ACT.Copy):
                return nc.scalar.activation(out, in_, func)
            for n in range(2 * KC):
                act.wait_ge(s["kv_t"], n + 1)
                dst = (kH, vH)[n // KC]
                high(dst[:, (n % KC) * KC:(n % KC + 1) * KC, :], kv[n % 2].rearrange("p (a c) -> p a c", a=KC)).then_inc(s["kvH"], 1)

            def q_high(g, t, h):
                act.wait_ge(s["xt"], t + 1)
                high(qH[:, bass.ds(g % 2, 1), :, h * P:(h + 1) * P].rearrange("p o h c -> p (o h) c"),
                     pX[:, :, :]).then_inc(s["qH"], 1)
            for t in range(GT):
                q_high(0, t, t)

            def out_copy(k, h):
                act.wait_ge(s["pv"], NPAIR * (k + 1))
                act.wait_ge(s["ot"], k) if not (isinstance(k, int) and k == 0) else None
                high(oT[:, :], pO[h % 2][:, :]).then_inc(s["oT"], 1)

            def body(g, first, last):
                for h in range(NH):
                    k = g * NH + h
                    for c in range(NPAIR):
                        n = NPAIR * k + c
                        early = first and h == 0
                        act.wait_ge(s["score"], n + 1)
                        if not (early and c < 2):
                            act.wait_ge(s["p"], n - 1)
                        high(r[:, c % 2, :, :], pS[c % 2][:, :, :], ACT.Relu).then_inc(s["relu"], 1)
                        act.wait_ge(s["relu"], n + 1)
                        if not (early and c < 4):
                            act.wait_ge(s["pv"], n - 3)
                        high(pH[:, c % 4, :, :], r[:, c % 2, :, :], ACT.Square).then_inc(s["pH"], 1)
                        if c == 2 and not early:
                            out_copy(k - 1, (h - 1) % NH)
                        if c == 6 and not last:
                            q_high(g + 1, k + GT, h)
            groups(act, body)
            out_copy(GROUPS * NH - 1, NH - 1)

        @block.vector
        def _(dve):
            link = Link(dve, s["own_dve"])
            for n in range(2 * KC):
                dve.wait_ge(s["kvH"], n + 1)
                high, low = ((kH, kL), (vH, vL))[n // KC]
                m = slice((n % KC) * KC, (n % KC + 1) * KC)
                nc.vector.tensor_tensor(low[:, m, :], kv[n % 2].rearrange("p (a c) -> p a c", a=KC),
                                        high[:, m, :].bitcast(F32), ALU.subtract).then_inc(s["kvL"], 1)
            for t in range(TILES):
                dve.wait_ge(s[f"stat_in{t // GT % 2}"], 16 * (t // GT // 2 + 1))
                nc.vector.bn_stats(out=st[:, t, :], in_=xg[:, t // GT % 2, t % GT, :]).then_inc(s["stat"], 1)
            dve.wait_ge(s["stat"], TILES)
            for t in range(TILES - 1):
                nc.vector.bn_aggr(out=mv[:, t, :], in_=st[:, t, :])
            link(nc.vector.bn_aggr(out=mv[:, TILES - 1, :], in_=st[:, TILES - 1, :]))
            link(nc.vector.tensor_scalar(v1[:, :], mv[:, :, 1], EPS, None, ALU.add))
            rsqrt(nc, link, r1[:, :], tmp[:, :], v1[:, :], ALU, I32)
            link(nc.vector.tensor_tensor(tmp[:, :], r1[:, :], r1[:, :], ALU.mult))
            link(nc.vector.tensor_tensor(tmp[:, :], tmp[:, :], mv[:, :, 1], ALU.mult))
            link(nc.vector.tensor_scalar(v2[:, :], tmp[:, :], EPS, None, ALU.add))
            rsqrt(nc, link, r2[:, :], tmp[:, :], v2[:, :], ALU, I32)
            link(nc.vector.tensor_tensor(r2[:, :], r2[:, :], r1[:, :], ALU.mult))

            def prep(g, h, first):
                t = g * GT + h
                at = bass.ds(t, 1)
                dve.wait_ge(s[f"x_in{h % 2}"], 16 * (g * (GT // 2) + h // 2 + 1))
                if not first:
                    dve.wait_ge(s["based"], t)
                    dve.wait_ge(s["xt"], t)
                mean = mv[:, at, 0]
                nc.vector.tensor_scalar(y[:, :], xb[:, h % 2, :], mean, r1[:, at], ALU.subtract, ALU.mult).then_inc(s["prep"], 1)
                nc.vector.tensor_scalar(qn[:, :], xb[:, h % 2, :], mean, r2[:, at], ALU.subtract, ALU.mult).then_inc(s["prep"], 1)

            def q_low(g, t, h):
                dve.wait_ge(s["qH"], t + 1)
                at = (bass.ds(g % 2, 1), slice(None), slice(h * P, (h + 1) * P))
                nc.vector.tensor_tensor(qL[(slice(None), *at)].rearrange("p o h c -> p (o h) c"), pX[:, :, :],
                                        qH[(slice(None), *at)].rearrange("p o h c -> p (o h) c").bitcast(F32),
                                        ALU.subtract).then_inc(s["qL"], 1)
            for t in range(GT):
                prep(0, t, t == 0)
                q_low(0, t, t)

            def add_out(k, g, h, first):
                dve.wait_ge(s["ot"], k + 1)
                if not first:
                    dve.wait_ge(s[f"out{h % 2}"], 16 * (g * (NH // 2) + h // 2))
                nc.vector.tensor_tensor(o1[:, h % 2, :, :], pT[:, :, :],
                                        base[:, bass.ds(g % 2, 1), :, h * P:(h + 1) * P].rearrange("p o t c -> p (o t) c"),
                                        ALU.add).then_inc(s["o1"], 1)

            def out_stats(k, g, h):
                dve.wait_ge(s["o1"], k + 1)
                for i in range(GT):
                    nc.vector.bn_stats(out=stats[:, bass.ds(g * GT + i, 1), h, :].rearrange("p o s -> p (o s)"), in_=o1[:, h % 2, i, :])

            def body(g, first, last):
                for h in range(NH):
                    k = g * NH + h
                    for c in range(NPAIR):
                        n = NPAIR * k + c
                        early = first and h == 0
                        dve.wait_ge(s["relu"], n + 1)
                        if not (early and c < 2):
                            wait_low(dve, k, c - 2)
                        nc.vector.tensor_tensor(p[:, c % 2, :, :], r[:, c % 2, :, :], r[:, c % 2, :, :],
                                                ALU.mult).then_inc(s["p"], 1)
                        if c not in POOL_LOW:
                            dve.wait_ge(s["pH"], n + 1)
                            dve.wait_ge(s["p"], n + 1)
                            nc.vector.tensor_tensor(pL[:, c % 4, :, :], p[:, c % 2, :, :],
                                                    pH[:, c % 4, :, :].bitcast(F32), ALU.subtract).then_inc(s["lowD"], 1)
                        if c == 0 and not last:
                            prep(g + 1, h, False)
                        if c == 5 and not early:
                            add_out(k - 1, g if h else g - 1, (h - 1) % NH, first and h <= 2)
                        if c == 7 and not early:
                            out_stats(k - 1, g if h else g - 1, (h - 1) % NH)
                        if c == 6 and not last:
                            q_low(g + 1, k + GT, h)
            groups(dve, body)
            add_out(GROUPS * NH - 1, GROUPS - 1, NH - 1, False)
            out_stats(GROUPS * NH - 1, GROUPS - 1, NH - 1)

        @block.tensor
        def _(pe):
            pe.wait_ge(s["ident"], 1)
            pe.wait_ge(s["w_in"], 32)
            for n in range(2 * KC):
                if n >= 2:
                    pe.wait_ge(s["kvL"], n - 1)
                for cb in range(KC):
                    j = n % KC
                    src = wf[:, cb, j * P:(j + 1) * P] if n < KC else wp[:, j, cb * P:(cb + 1) * P]
                    t = nc.tensor.transpose(kv[n % 2][:, cb * P:(cb + 1) * P], src, ident[:, :])
                t.then_inc(s["kv_t"], 1)

            def x_transpose(t, first):
                pe.wait_ge(s["affined"], t + 1)
                if not first:
                    pe.wait_ge(s["qL"], t)
                for h in range(NH):
                    m = nc.tensor.transpose(pX[:, h, :], qn[:, h * P:(h + 1) * P], ident[:, :])
                m.then_inc(s["xt"], 1)
            for t in range(GT):
                x_transpose(t, t == 0)
            pe.wait_ge(s["kvL"], 2 * KC)

            def products(k, h, c):
                n = NPAIR * k + c
                pe.wait_ge(s["pH"], n + 1)
                wait_low(pe, k, c)
                for i in range(2):
                    m = 2 * c + i
                    last = split_matmuls(nc, pO[h % 2][:, :], (vH[:, m, :], vL[:, m, :]),
                                         (pH[:, c % 4, i, :], pL[:, c % 4, i, :]), m == 0, m == SC - 1)
                last.then_inc(s["pv"], 1)

            def out_transpose(k, first):
                pe.wait_ge(s["oT"], k + 1)
                if not first:
                    pe.wait_ge(s["o1"], k)
                for t in range(GT):
                    m = nc.tensor.transpose(pT[:, t, :], oT[:, t * P:(t + 1) * P], ident[:, :])
                m.then_inc(s["ot"], 1)

            def body(g, first, last):
                pe.wait_ge(s["qL"], GT * g + GT)
                for h in range(NH):
                    k = g * NH + h
                    for c in range(NPAIR):
                        n = NPAIR * k + c
                        early = first and h == 0
                        if not (early and c < 2):
                            pe.wait_ge(s["relu"], n - 1)
                        for i in range(2):
                            m = 2 * c + i
                            at = (bass.ds(g % 2, 1), h, slice(None))
                            last_m = split_matmuls(nc, pS[c % 2][:, i, :], (kH[:, m, :], kL[:, m, :]),
                                                   tuple(q[(slice(None), *at)].rearrange("p o c -> p (o c)") for q in (qH, qL)),
                                                   True, True)
                        last_m.then_inc(s["score"], 1)
                        if c >= 2:
                            if c == 2 and not (first and h < 2):
                                pe.wait_ge(s["oT"], k - 1)
                            products(k, h, c - 2)
                        elif not early:
                            products(k - 1, h - 1, c + NPAIR - 2)
                        if c == 4 and not early:
                            out_transpose(k - 1, first and h == 1)
                        if c == 5 and not last:
                            x_transpose(k + GT, False)
            groups(pe, body)
            for c in (NPAIR - 2, NPAIR - 1):
                products(GROUPS * NH - 1, NH - 1, c)
            out_transpose(GROUPS * NH - 1, False)


def wait(eng, sem, value):
    if not (isinstance(value, int) and value <= 0):
        eng.wait_ge(sem, value)


def split_weights(nc, ctx, tag, parts, mybir):
    F32 = mybir.dt.float32
    SLOTS = 3
    stage = ctx.enter_context(nc.sbuf_tensor(tag + "stage", [128, SLOTS, 1024], F32))
    arrived = [ctx.enter_context(nc.semaphore(f"{tag}w_in{i}")) for i in range(SLOTS)]
    high_done = ctx.enter_context(nc.semaphore(tag + "w_high"))
    low_done = ctx.enter_context(nc.semaphore(tag + "w_low"))

    def shaped(ap, like):
        return ap.rearrange("p (a b) -> p a b", b=like.shape[-1]) if len(like.shape) == 3 else ap

    def load(sp):
        for n, (src, hi, lo) in enumerate(parts):
            wait(sp, low_done, n + 1 - SLOTS)
            sp.dma_start(shaped(stage[:, n % SLOTS, :], src), src).then_inc(arrived[n % SLOTS], 16)

    def high(act, lo=0, up=None):
        for n, (src, hi, _) in enumerate(parts):
            act.wait_ge(arrived[n % SLOTS], 16 * (n // SLOTS + 1))
            nc.scalar.activation(hi, shaped(stage[:, n % SLOTS, :], hi), mybir.ActivationFunctionType.Copy).then_inc(high_done, 1)

    def low(dve):
        for n, (src, hi, lo) in enumerate(parts):
            dve.wait_ge(high_done, n + 1)
            nc.vector.tensor_tensor(lo, shaped(stage[:, n % SLOTS, :], lo), hi.bitcast(F32),
                                    mybir.AluOpType.subtract).then_inc(low_done, 1)
    return load, high, low, low_done


def layernorm_stats(nc, link, stats, parts, mv, var, tmp, rstd, mybir):
    ALU = mybir.AluOpType
    n = stats.shape[1]
    for t in range(n):
        m = nc.vector.bn_aggr(out=mv[:, t, :], in_=stats[:, t, 0:parts, :])
    link(m)
    link(nc.vector.tensor_scalar(var[:, :], mv[:, :, 1], EPS, None, ALU.add))
    rsqrt(nc, link, rstd[:, :], tmp[:, :], var[:, :], ALU, mybir.dt.int32)


def cross_attention(nc, ident, stats, x1, ctx_in, mask, Wq, Wk, Wv, Wo, x2, mybir, bass, ExitStack):
    F32, F32R, U8 = mybir.dt.float32, mybir.dt.float32r, mybir.dt.uint8
    ALU, ACT, AX = mybir.AluOpType, mybir.ActivationFunctionType, mybir.AxisListType
    HD = 64
    INNER = Wq.shape[1]
    NPAIR = INNER // P
    KEYS = ctx_in.shape[1]
    SCALE = HD ** -0.5
    FMAX = 3.4028234663852886e38
    ROWT = mask.shape[0] // P
    BG = GROUPS // NB
    SUB = 2 * GT
    x1_t = x1.rearrange("(t p) c -> p t c", p=P)
    x2_t = x2.rearrange("(t p) c -> p t c", p=P)
    with ExitStack() as keep:
        sbk = lambda n, s, d=F32: keep.enter_context(nc.sbuf_tensor("b_" + n, s, d))
        kH, kL = (sbk(n, [P, NPAIR, NB, KEYS], F32R) for n in ("kH", "kL"))
        vH, vL = (sbk(n, [KEYS, NB, NPAIR, 2, P], F32R) for n in ("vH", "vL"))
        wqH, wqL = (sbk(n, [P, KC, INNER], F32R) for n in ("wqH", "wqL"))
        woH, woL = (sbk(n, [P, NPAIR, C], F32R) for n in ("woH", "woL"))
        mv, rstd = sbk("mv", [P, TILES, 2]), sbk("rstd", [P, TILES])

        with ExitStack() as ctx:
            sb = lambda n, s, d=F32: ctx.enter_context(nc.sbuf_tensor("b_" + n, s, d))
            ps = lambda n, s: ctx.enter_context(nc.psum_tensor("b_" + n, s, F32))
            wkH, wkL = (sb(n, [P, KC, INNER], F32R) for n in ("wkH", "wkL"))
            wvH, wvL = (sb(n, [P, KC, INNER], F32R) for n in ("wvH", "wvL"))
            cx = sb("cx", [KEYS, NB, C])
            cH, cL = (sb(n, [P, KC, NB, KEYS], F32R) for n in ("cH", "cL"))
            var, tmp = sb("var", [P, TILES]), sb("tmp", [P, TILES])
            pC = [ps(f"pC{i}", [P, 2, NB, KEYS]) for i in range(2)]
            pK = [ps(f"pK{i}", [P, NB, KEYS]) for i in range(2)]
            pV = [ps(f"pV{i}", [KEYS, NPAIR // 2, 2, HD]) for i in range(2)]
            s = {n: ctx.enter_context(nc.semaphore("bs_" + n)) for n in
                 "c_in own zero ct cH cL k_ps kH kL v_ps vH vL".split()}
            parts = []
            for w, hi, lo in ((Wk, wkH, wkL), (Wv, wvH, wvL), (Wq, wqH, wqL)):
                w_v = w.rearrange("(a p) n -> p a n", p=P)
                parts += [(w_v[:, a, :], hi[:, a, :], lo[:, a, :]) for a in range(KC)]
            wo_v = Wo.rearrange("(a p) n -> p a n", p=P)
            parts += [(wo_v[:, a:a + 2, :], woH[:, a:a + 2, :], woL[:, a:a + 2, :]) for a in range(0, NPAIR, 2)]
            load, high, low, low_done = split_weights(nc, ctx, "bs_", parts, mybir)
            block = ctx.enter_context(nc.Block())

            @block.sync
            def _(sp):
                sp.dma_start(cx[:, :, :], ctx_in.rearrange("b k c -> k b c")).then_inc(s["c_in"], 16)
                load(sp)

            @block.gpsimd
            def _(pool):
                nc.gpsimd.memset(vH[:, :, :, :, :].bitcast(F32), 0.0).then_inc(s["zero"], 1)
                nc.gpsimd.memset(vL[:, :, :, :, :].bitcast(F32), 0.0).then_inc(s["zero"], 1)

            @block.scalar
            def _(act):
                copy = lambda out, in_: nc.scalar.activation(out, in_, ACT.Copy)
                for i in range(2):
                    act.wait_ge(s["ct"], i + 1)
                    copy(cH[:, 2 * i:2 * i + 2, :, :], pC[i][:, :, :, :]).then_inc(s["cH"], 1)
                high(act)
                for j in range(NPAIR):
                    act.wait_ge(s["k_ps"], j + 1)
                    copy(kH[:, j, :, :], pK[j % 2][:, :, :]).then_inc(s["kH"], 1)
                act.wait_ge(s["zero"], 2)
                for n in range(2 * NB):
                    act.wait_ge(s["v_ps"], n + 1)
                    b, half = divmod(n, 2)
                    for i in range(2):
                        m = copy(vH[:, b, half * NPAIR // 2:(half + 1) * NPAIR // 2, i, i * HD:(i + 1) * HD], pV[n % 2][:, :, i, :])
                    m.then_inc(s["vH"], 1)

            @block.vector
            def _(dve):
                link = Link(dve, s["own"])
                sub = lambda out, in_, hi: nc.vector.tensor_tensor(out, in_, hi.bitcast(F32), ALU.subtract)
                for i in range(2):
                    dve.wait_ge(s["cH"], i + 1)
                    sub(cL[:, 2 * i:2 * i + 2, :, :], pC[i][:, :, :, :], cH[:, 2 * i:2 * i + 2, :, :]).then_inc(s["cL"], 1)
                layernorm_stats(nc, link, stats, KC, mv, var, tmp, rstd, mybir)
                low(dve)
                for j in range(NPAIR):
                    dve.wait_ge(s["kH"], j + 1)
                    sub(kL[:, j, :, :], pK[j % 2][:, :, :], kH[:, j, :, :]).then_inc(s["kL"], 1)
                dve.wait_ge(s["zero"], 2)
                for n in range(2 * NB):
                    dve.wait_ge(s["vH"], n + 1)
                    b, half = divmod(n, 2)
                    for i in range(2):
                        at = (slice(None), b, slice(half * NPAIR // 2, (half + 1) * NPAIR // 2), i, slice(i * HD, (i + 1) * HD))
                        m = sub(vL[at], pV[n % 2][:, :, i, :], vH[at])
                    m.then_inc(s["vL"], 1)

            @block.tensor
            def _(pe):
                pe.wait_ge(s["c_in"], 16)
                for a in range(KC):
                    for b in range(NB):
                        m = nc.tensor.transpose(pC[a // 2][:, a % 2, b, :], cx[:, b, a * P:(a + 1) * P], ident[:, :])
                    if a % 2:
                        m.then_inc(s["ct"], 1)
                pe.wait_ge(s["cL"], 2)
                pe.wait_ge(low_done, KC)
                for j in range(NPAIR):
                    wait(pe, s["kL"], j - 1)
                    for a in range(KC):
                        at = (slice(None), a, slice(j * P, (j + 1) * P))
                        m = split_matmuls(nc, pK[j % 2][:, :, :], (wkH[at], wkL[at]), (cH[:, a, :, :], cL[:, a, :, :]), a == 0, a == KC - 1)
                    m.then_inc(s["k_ps"], 1)
                pe.wait_ge(low_done, 2 * KC)
                for n in range(2 * NB):
                    wait(pe, s["vL"], n - 1)
                    b, half = divmod(n, 2)
                    for a in range(KC):
                        at = (slice(None), a, slice(half * INNER // 2, (half + 1) * INNER // 2))
                        m = split_matmuls(nc, pV[n % 2][:, :, :, :].rearrange("p a i d -> p (a i d)"), (cH[:, a, b, :], cL[:, a, b, :]),
                                          (wvH[at], wvL[at]), a == 0, a == KC - 1)
                    m.then_inc(s["v_ps"], 1)

        with ExitStack() as ctx:
            sb = lambda n, s, d=F32: ctx.enter_context(nc.sbuf_tensor("b_" + n, s, d))
            ps = lambda n, s: ctx.enter_context(nc.psum_tensor("b_" + n, s, F32))
            mu = sb("mu", [P, ROWT, KEYS], U8)
            bias = sb("bias", [P, GT, KEYS])
            xb, xn = sb("xb", [P, 2, C]), sb("xn", [P, 2, C])
            xr = sb("xr", [P, 2, C])
            xH, xL = (sb(n, [P, KC, GTOK], F32R) for n in ("xH", "xL"))
            qH, qL = (sb(n, [P, 2, GTOK], F32R) for n in ("qH", "qL"))
            S = sb("S", [P, 2, SUB, KEYS])
            nm, rs, ri = (sb(n, [P, 2, SUB]) for n in ("nm", "rs", "ri"))
            tH, tL = (sb(n, [KEYS, 2, GTOK], F32R) for n in ("tH", "tL"))
            aH, aL = (sb(n, [P, NPAIR, GTOK], F32R) for n in ("aH", "aL"))
            pQ, pS = ps("pQ", [P, GTOK]), ps("pS", [P, 2, GT, KEYS])
            pT, pO = ps("pT", [KEYS, 2, GTOK]), ps("pO", [P, GTOK])
            pY = [ps(f"pY{i}", [P, C])[:, :] for i in range(2)]
            pX = [y.rearrange("p (a c) -> p a c", c=P) for y in pY]
            s = {n: ctx.enter_context(nc.semaphore("b_" + n)) for n in
                 ("m_in x_in0 x_in1 r_in0 r_in1 bias normed xt xH xL q_ps qH qL score masked nmax exp rinv prob"
                  " tp tH tL pv aH aL wo res seen out0 out1").split()}

            def groups(eng, body):
                for b in range(NB):
                    body(b * BG, b, max(b - 1, 0), b == 0, False)
                    end = (b + 1) * BG - (b == NB - 1)
                    with eng.Fori(b * BG + 1, end) as g:
                        body(g, b, b, False, False)
                body(GROUPS - 1, NB - 1, NB - 1, False, True)

            block = ctx.enter_context(nc.Block())

            @block.sync
            def _(sp):
                sp.dma_start(mu[:, :, :], mask.rearrange("(t p) k -> p t k", p=P)).then_inc(s["m_in"], 16)

                def load(t, i):
                    sp.dma_start(xb[:, i % 2, :], x1_t[:, bass.ds(t, 1), :].rearrange("p o c -> p (o c)")).then_inc(s[f"x_in{i % 2}"], 16)

                def free(g, i):
                    sp.wait_ge(s["seen"], g * GT + i + 1)
                    sp.wait_ge(s[f"out{i % 2}"], 16 * (g * (GT // 2) + i // 2 + 1))

                def reload(g, i):
                    t = g * GT + i
                    if i >= 2:
                        free(g, i - 2)
                    sp.dma_start(xr[:, i % 2, :], x1_t[:, bass.ds(t, 1), :].rearrange("p o c -> p (o c)")).then_inc(s[f"r_in{i % 2}"], 16)

                def store(t, i):
                    sp.wait_ge(s["res"], t + 1)
                    sp.dma_start(x2_t[:, bass.ds(t, 1), :].rearrange("p o c -> p (o c)"), xr[:, i % 2, :]).then_inc(s[f"out{i % 2}"], 16)

                def outputs(g):
                    for i in range(GT):
                        reload(g, i)
                        if i:
                            store(g * GT + i - 1, i - 1)
                    store(g * GT + GT - 1, GT - 1)
                    for i in range(GT - 2, GT):
                        free(g, i)
                for i in range(GT):
                    wait(sp, s["normed"], i - 1)
                    load(i, i)

                def body(g, b, pb, first, last):
                    if not first:
                        outputs(g - 1)
                    if not last:
                        for i in range(GT):
                            sp.wait_ge(s["normed"], g * GT + GT + i - 1)
                            load(g * GT + GT + i, i)
                groups(sp, body)
                outputs(GROUPS - 1)

            @block.gpsimd
            def _(pool):
                def body(g, b, pb, first, last):
                    for j in range(NPAIR):
                        n = NPAIR * g + j
                        pool.wait_ge(s["rinv"], n + 1)
                        nc.gpsimd.tensor_tensor(S[:, j % 2, :, :], S[:, j % 2, :, :],
                                                ri[:, j % 2, :].unsqueeze(2).to_broadcast([P, SUB, KEYS]), ALU.mult).then_inc(s["prob"], 1)
                groups(pool, body)

            @block.scalar
            def _(act):
                def x_high(t, i):
                    act.wait_ge(s["xt"], t + 1)
                    nc.scalar.activation(xH[:, :, i * P:(i + 1) * P], pX[i % 2], ACT.Copy).then_inc(s["xH"], 1)

                def q_high(m, j):
                    act.wait_ge(s["q_ps"], m + 1)
                    wait(act, s["score"], m - 1)
                    nc.scalar.activation(qH[:, j % 2, :], pQ[:, :], ACT.Copy, scale=SCALE).then_inc(s["qH"], 1)

                def exps(m, j):
                    act.wait_ge(s["nmax"], m + 1)
                    for i in range(SUB):
                        e = nc.scalar.activation(S[:, j % 2, i, :], S[:, j % 2, i, :], ACT.Exp,
                                                 bias=nm[:, j % 2, i:i + 1], accum_out=rs[:, j % 2, i:i + 1])
                    e.then_inc(s["exp"], 1)

                def t_high(m):
                    act.wait_ge(s["tp"], m + 1)
                    wait(act, s["pv"], m)
                    nc.scalar.activation(tH[:, :, :], pT[:, :, :], ACT.Copy).then_inc(s["tH"], 1)

                def a_high(m, g, j):
                    act.wait_ge(s["pv"], m + 1)
                    wait(act, s["wo"], GT * g)
                    nc.scalar.activation(aH[:, j, :], pO[:, :], ACT.Copy).then_inc(s["aH"], 1)
                for i in range(GT):
                    x_high(i, i)
                q_high(0, 0)

                def body(g, b, pb, first, last):
                    for j in range(NPAIR):
                        n = NPAIR * g + j
                        if j < NPAIR - 1:
                            q_high(n + 1, j + 1)
                        if not last:
                            for i in {NPAIR - 2: (0, 1), NPAIR - 1: (2, 3)}.get(j, ()):
                                x_high(GT * g + GT + i, i)
                        if j > 1 or not first:
                            a_high(n - 2, g if j > 1 else g - 1, (j - 2) % NPAIR)
                        if j == NPAIR - 1 and not last:
                            q_high(n + 1, 0)
                        if j or not first:
                            t_high(n - 1)
                        exps(n, j)
                groups(act, body)
                n = NPAIR * GROUPS
                a_high(n - 2, GROUPS - 1, NPAIR - 2)
                t_high(n - 1)
                a_high(n - 1, GROUPS - 1, NPAIR - 1)

            @block.vector
            def _(dve):
                sub = lambda out, in_, hi: nc.vector.tensor_tensor(out, in_, hi.bitcast(F32), ALU.subtract)

                def norm(g, i):
                    t = g * GT + i
                    at = bass.ds(t, 1)
                    dve.wait_ge(s[f"x_in{i % 2}"], 16 * (g * (GT // 2) + i // 2 + 1))
                    wait(dve, s["xt"], t - 1)
                    nc.vector.tensor_scalar(xn[:, i % 2, :], xb[:, i % 2, :], mv[:, at, 0], rstd[:, at],
                                            ALU.subtract, ALU.mult).then_inc(s["normed"], 1)

                def x_low(t, i):
                    dve.wait_ge(s["xH"], t + 1)
                    at = (slice(None), slice(None), slice(i * P, (i + 1) * P))
                    sub(xL[at], pX[i % 2], xH[at]).then_inc(s["xL"], 1)

                def q_low(m, j):
                    dve.wait_ge(s["qH"], m + 1)
                    nc.vector.scalar_tensor_tensor(out=qL[:, j % 2, :], in0=pQ[:, :], scalar=SCALE, in1=qH[:, j % 2, :].bitcast(F32),
                                                   op0=ALU.mult, op1=ALU.subtract).then_inc(s["qL"], 1)

                def add_mask(m, g, j):
                    dve.wait_ge(s["score"], m + 1)
                    wait(dve, s["tp"], m - 1)
                    if j == 0:
                        nc.vector.tensor_scalar(bias[:, :, :], mu[:, bass.ds((g % BG) * GT, GT), :],
                                                -1.0, FMAX, ALU.add, ALU.mult).then_inc(s["bias"], 1)
                        dve.wait_ge(s["bias"], g + 1)
                    nc.vector.tensor_tensor(S[:, j % 2, :, :].rearrange("p (i t) k -> p i (t k)", i=2),
                                            pS[:, :, :, :].rearrange("p i t k -> p i (t k)"),
                                            bias[:, :, :].rearrange("p (o t) k -> p o (t k)", o=1).to_broadcast([P, 2, GT * KEYS]),
                                            ALU.add).then_inc(s["masked"], 1)

                def maximum(m, j):
                    dve.wait_ge(s["masked"], m + 1)
                    nc.vector.tensor_reduce(nm[:, j % 2, :], S[:, j % 2, :, :], axis=AX.X, op=ALU.max, negate=True).then_inc(s["nmax"], 1)

                def inverse(m, j):
                    dve.wait_ge(s["exp"], m + 1)
                    nc.vector.reciprocal(ri[:, j % 2, :], rs[:, j % 2, :]).then_inc(s["rinv"], 1)

                def t_low(m):
                    dve.wait_ge(s["tH"], m + 1)
                    sub(tL[:, :, :], pT[:, :, :], tH[:, :, :]).then_inc(s["tL"], 1)

                def a_low(m, j):
                    dve.wait_ge(s["aH"], m + 1)
                    sub(aL[:, j, :], pO[:, :], aH[:, j, :]).then_inc(s["aL"], 1)

                def add(g, i):
                    t = g * GT + i
                    dve.wait_ge(s["wo"], t + 1)
                    dve.wait_ge(s[f"r_in{i % 2}"], 16 * (g * (GT // 2) + i // 2 + 1))
                    nc.vector.tensor_tensor(xr[:, i % 2, :], pY[i % 2], xr[:, i % 2, :], ALU.add).then_inc(s["res"], 1)

                def out_stats(g, i):
                    t = g * GT + i
                    dve.wait_ge(s["res"], t + 1)
                    nc.vector.bn_stats(out=stats[:, bass.ds(t, 1), 0, :].rearrange("p o s -> p (o s)"), in_=xr[:, i % 2, :]).then_inc(s["seen"], 1)

                def outputs(g):
                    for i in range(GT):
                        add(g, i)
                        if i:
                            out_stats(g, i - 1)
                    out_stats(g, GT - 1)
                dve.wait_ge(s["m_in"], 16)
                norm(0, 0)
                norm(0, 1)
                for i in range(GT):
                    x_low(i, i)
                    if i + 2 < GT:
                        norm(0, i + 2)
                q_low(0, 0)

                def body(g, b, pb, first, last):
                    for j in range(NPAIR):
                        n = NPAIR * g + j
                        add_mask(n, g, j)
                        if j or not first:
                            inverse(n - 1, (j - 1) % NPAIR)
                        maximum(n, j)
                        if j < NPAIR - 1:
                            q_low(n + 1, j + 1)
                        if not last:
                            for i in {NPAIR - 2: (0, 1), NPAIR - 1: (2, 3)}.get(j, ()):
                                x_low(GT * g + GT + i, i)
                        if j > 1 or not first:
                            a_low(n - 2, (j - 2) % NPAIR)
                        if j == NPAIR - 1 and not last:
                            q_low(n + 1, 0)
                        if j or not first:
                            t_low(n - 1)
                        if j == 1 and not first:
                            outputs(g - 1)
                        if not last:
                            for i in {NPAIR - 4: (0, 1), NPAIR - 2: (2, 3)}.get(j, ()):
                                norm(g + 1, i)
                groups(dve, body)
                n = NPAIR * GROUPS
                inverse(n - 1, NPAIR - 1)
                a_low(n - 2, NPAIR - 2)
                t_low(n - 1)
                a_low(n - 1, NPAIR - 1)
                outputs(GROUPS - 1)

            @block.tensor
            def _(pe):
                def x_transpose(t, i, g):
                    pe.wait_ge(s["normed"], t + 1)
                    if i < 2:
                        wait(pe, s["res"], GT * (g - 1))
                    else:
                        pe.wait_ge(s["xL"], t - 1)
                    for a in range(KC):
                        m = nc.tensor.transpose(pX[i % 2][:, a, :], xn[:, i % 2, a * P:(a + 1) * P], ident[:, :])
                    m.then_inc(s["xt"], 1)

                def query(m, j):
                    wait(pe, s["qL"], m)
                    for a in range(KC):
                        at = (slice(None), a, slice(j * P, (j + 1) * P))
                        last = split_matmuls(nc, pQ[:, :], (wqH[at], wqL[at]), (xH[:, a, :], xL[:, a, :]), a == 0, a == KC - 1)
                    last.then_inc(s["q_ps"], 1)

                def scores(m, b, j):
                    pe.wait_ge(s["qL"], m + 1)
                    wait(pe, s["masked"], m)
                    for t in range(GT):
                        for i in range(2):
                            row = slice(i * HD, (i + 1) * HD)
                            q_at = (row, j % 2, slice(t * P, (t + 1) * P))
                            last = split_matmuls(nc, pS[:, i, t, :], (qH[q_at], qL[q_at]), (kH[row, j, b, :], kL[row, j, b, :]), True, True)
                    last.then_inc(s["score"], 1)

                def p_transpose(m, j):
                    pe.wait_ge(s["prob"], m + 1)
                    wait(pe, s["tL"], m)
                    for i in range(2):
                        for t in range(GT):
                            last = nc.tensor.transpose(pT[:, i, t * P:(t + 1) * P], S[:, j % 2, i * GT + t, :], ident[:, :])
                    last.then_inc(s["tp"], 1)

                def values(m, b, j):
                    pe.wait_ge(s["tL"], m + 1)
                    wait(pe, s["aL"], m)
                    for i in range(2):
                        last = split_matmuls(nc, pO[:, :], (vH[:, b, j, i, :], vL[:, b, j, i, :]), (tH[:, i, :], tL[:, i, :]), i == 0, i == 1)
                    last.then_inc(s["pv"], 1)

                def project(g, i):
                    t = g * GT + i
                    pe.wait_ge(s["aL"], NPAIR * g + NPAIR - 1)
                    if i >= 2:
                        pe.wait_ge(s["res"], t - 1)
                    for j in range(NPAIR):
                        if j == NPAIR - 1:
                            pe.wait_ge(s["aL"], NPAIR * g + NPAIR)
                        at = (slice(None), j, slice(i * P, (i + 1) * P))
                        last = split_matmuls(nc, pY[i % 2], (aH[at], aL[at]), (woH[:, j, :], woL[:, j, :]), j == 0, j == NPAIR - 1)
                    last.then_inc(s["wo"], 1)
                for i in range(GT):
                    x_transpose(i, i, 0)
                pe.wait_ge(s["xL"], GT)
                query(0, 0)

                def body(g, b, pb, first, last):
                    for j in range(NPAIR):
                        n = NPAIR * g + j
                        turn = GT * g + GT
                        scores(n, b, j)
                        if j < NPAIR - 1:
                            query(n + 1, j + 1)
                        elif not last:
                            x_transpose(turn + 2, 2, g + 1)
                            x_transpose(turn + 3, 3, g + 1)
                        if j > 1 or not first:
                            values(n - 2, b if j > 1 else pb, (j - 2) % NPAIR)
                        if j == NPAIR - 1 and not last:
                            pe.wait_ge(s["xL"], turn + GT)
                            query(n + 1, 0)
                        if j or not first:
                            p_transpose(n - 1, (j - 1) % NPAIR)
                        if j == 1 and not first:
                            for i in range(GT):
                                project(g - 1, i)
                        if j == NPAIR - 3 and not last:
                            x_transpose(turn, 0, g + 1)
                            x_transpose(turn + 1, 1, g + 1)
                groups(pe, body)
                n = NPAIR * GROUPS
                values(n - 2, NB - 1, NPAIR - 2)
                p_transpose(n - 1, NPAIR - 1)
                values(n - 1, NB - 1, NPAIR - 1)
                for i in range(GT):
                    project(GROUPS - 1, i)


def shared_experts(nc, ident, stats, x2, gate_w, Wg, Wu, Wd, onehot, xs, base_out, mybir, bass, ExitStack):
    F32, F32R = mybir.dt.float32, mybir.dt.float32r
    ALU, ACT, AX = mybir.AluOpType, mybir.ActivationFunctionType, mybir.AxisListType
    EXP = gate_w.shape[1]
    IC = Wg.shape[1] // P
    x2_t, xs_t, out_t = (a.rearrange("(t p) c -> p t c", p=P) for a in (x2, xs, base_out))
    with ExitStack() as keep:
        sbk = lambda n, s, d=F32: keep.enter_context(nc.sbuf_tensor("c_" + n, s, d))
        wgH, wgL, wuH, wuL = (sbk(n, [P, KC, IC * P], F32R) for n in ("wgH", "wgL", "wuH", "wuL"))
        wdH, wdL = (sbk(n, [P, IC, C], F32R) for n in ("wdH", "wdL"))
        rH, rL = (sbk(n, [P, KC, EXP], F32R) for n in ("rH", "rL"))
        desc = sbk("desc", [P, EXP])
        mv, rstd = sbk("mv", [P, TILES, 2]), sbk("rstd", [P, TILES])

        with ExitStack() as ctx:
            sb = lambda n, s, d=F32: ctx.enter_context(nc.sbuf_tensor("c_" + n, s, d))
            var, tmp = sb("var", [P, TILES]), sb("tmp", [P, TILES])
            rw, ramp = sb("rw", [P, KC, EXP]), sb("ramp", [P, EXP], mybir.dt.int32)
            s = {n: ctx.enter_context(nc.semaphore("cs_" + n)) for n in "ramp r_in own rH".split()}
            parts = []
            for w, hi, lo in ((Wg, wgH, wgL), (Wu, wuH, wuL)):
                w_v = w.rearrange("(a p) n -> p a n", p=P)
                parts += [(w_v[:, a, :], hi[:, a, :], lo[:, a, :]) for a in range(KC)]
            wd_v = Wd.rearrange("(a p) n -> p a n", p=P)
            parts += [(wd_v[:, a:a + 2, :], wdH[:, a:a + 2, :], wdL[:, a:a + 2, :]) for a in range(0, IC, 2)]
            load, high, low, _ = split_weights(nc, ctx, "cs_", parts, mybir)
            block = ctx.enter_context(nc.Block())

            @block.sync
            def _(sp):
                sp.dma_start(rw[:, :, :], gate_w.rearrange("(a p) n -> p a n", p=P)).then_inc(s["r_in"], 16)
                load(sp)

            @block.gpsimd
            def _(pool):
                nc.gpsimd.iota(ramp[:, :], pattern=[[-1, EXP]], base=EXP, channel_multiplier=0).then_inc(s["ramp"], 1)

            @block.scalar
            def _(act):
                act.wait_ge(s["r_in"], 16)
                nc.scalar.activation(rH[:, :, :], rw[:, :, :], ACT.Copy).then_inc(s["rH"], 1)
                high(act)

            @block.vector
            def _(dve):
                link = Link(dve, s["own"])
                dve.wait_ge(s["ramp"], 1)
                nc.vector.tensor_copy(desc[:, :], ramp[:, :])
                dve.wait_ge(s["rH"], 1)
                nc.vector.tensor_tensor(rL[:, :, :], rw[:, :, :], rH[:, :, :].bitcast(F32), ALU.subtract)
                layernorm_stats(nc, link, stats, 1, mv, var, tmp, rstd, mybir)
                low(dve)

        with ExitStack() as ctx:
            sb = lambda n, s, d=F32: ctx.enter_context(nc.sbuf_tensor("c_" + n, s, d))
            ps = lambda n, s: ctx.enter_context(nc.psum_tensor("c_" + n, s, F32))
            xb, x3 = sb("xb", [P, 2, C]), sb("x3", [P, GT, C])
            xr, o3, xo = sb("xr", [P, 2, C]), sb("o3", [P, 2, C]), sb("xo", [P, GT, C])
            xH, xL = (sb(n, [P, KC, GTOK], F32R) for n in ("xH", "xL"))
            sg, h = sb("sg", [P, 2, GTOK]), sb("h", [P, 2, GTOK])
            hH, hL = (sb(n, [P, IC, GTOK], F32R) for n in ("hH", "hL"))
            top, score, first_of = sb("top", [P, GT]), sb("score", [P, GT]), sb("first_of", [P, GT])
            rank = sb("rank", [P, GT, EXP])
            pG = [ps(f"pG{i}", [P, GTOK]) for i in range(2)]
            pU = [ps(f"pU{i}", [P, GTOK]) for i in range(2)]
            pD = [ps(f"pD{i}", [P, C]) for i in range(2)]
            pX, pR = ps("pX", [P, KC, P]), ps("pR", [P, GT, EXP])
            s = {n: ctx.enter_context(nc.semaphore("c_" + n)) for n in
                 "x_in0 x_in1 r_in0 r_in1 normed xt xH xL gate up sig gated h hH hL logit top own score xs xs_out down sum out0 out1".split()}
            RL = 4

            def groups(eng, body):
                body(0, True, False)
                with eng.Fori(1, GROUPS - 1) as g:
                    body(g, False, False)
                body(GROUPS - 1, False, True)

            block = ctx.enter_context(nc.Block())
            row = lambda a, t: a[:, bass.ds(t, 1), :].rearrange("p o c -> p (o c)")

            @block.sync
            def _(sp):
                def load(t, i):
                    sp.dma_start(xb[:, i % 2, :], row(x2_t, t)).then_inc(s[f"x_in{i % 2}"], 16)
                for i in range(GT):
                    wait(sp, s["normed"], i - 1)
                    load(i, i)

                def body(g, first, last):
                    sp.wait_ge(s["xs"], g + 1)
                    sp.dma_start(xs_t[:, bass.ds(g * GT, GT), :], xo[:, :, :]).then_inc(s["xs_out"], 16)
                    for i in range(GT):
                        t = g * GT + i
                        if not last:
                            sp.wait_ge(s["normed"], t + GT - 1)
                            load(t + GT, i)
                        wait(sp, s["sum"], t - 1)
                        sp.dma_start(xr[:, i % 2, :], row(x2_t, t)).then_inc(s[f"r_in{i % 2}"], 16)
                        if i:
                            store(t - 1, i - 1)
                    store(t, GT - 1)

                def store(t, i):
                    sp.wait_ge(s["sum"], t + 1)
                    sp.dma_start(row(out_t, t), o3[:, i % 2, :]).then_inc(s[f"out{i % 2}"], 16)
                groups(sp, body)
                sp.wait_ge(s["xs_out"], 16 * GROUPS)
                for i in range(2):
                    sp.wait_ge(s[f"out{i}"], 16 * TILES // 2)

            @block.scalar
            def _(act):
                def x_high(t, i):
                    act.wait_ge(s["xt"], t + 1)
                    nc.scalar.activation(xH[:, :, i * P:(i + 1) * P], pX[:, :, :], ACT.Copy).then_inc(s["xH"], 1)
                for i in range(GT):
                    x_high(i, i)

                def body(g, first, last):
                    for i in range(IC):
                        n = IC * g + i
                        act.wait_ge(s["gate"], n + 1)
                        wait(act, s["h"], n - 1)
                        nc.scalar.activation(sg[:, i % 2, :], pG[i % 2][:, :], ACT.Sigmoid).then_inc(s["sig"], 1)
                        if i == 1:
                            act.wait_ge(s["top"], g + 1)
                            nc.scalar.activation(score[:, :], top[:, :], ACT.Sigmoid).then_inc(s["score"], 1)
                        act.wait_ge(s["h"], n + 1)
                        if i == 0:
                            wait(act, s["down"], GT * g)
                        nc.scalar.activation(hH[:, i, :], h[:, i % 2, :], ACT.Copy).then_inc(s["hH"], 1)
                    if not last:
                        for i in range(GT):
                            x_high(GT * g + GT + i, i)
                groups(act, body)

            @block.vector
            def _(dve):
                sub = lambda out, in_, hi: nc.vector.tensor_tensor(out, in_, hi.bitcast(F32), ALU.subtract)

                def norm(g, i):
                    t = g * GT + i
                    at = bass.ds(t, 1)
                    dve.wait_ge(s[f"x_in{i % 2}"], 16 * (g * (GT // 2) + i // 2 + 1))
                    nc.vector.tensor_scalar(x3[:, i, :], xb[:, i % 2, :], mv[:, at, 0], rstd[:, at],
                                            ALU.subtract, ALU.mult).then_inc(s["normed"], 1)

                def x_low(t, i):
                    dve.wait_ge(s["xH"], t + 1)
                    at = (slice(None), slice(None), slice(i * P, (i + 1) * P))
                    sub(xL[at], pX[:, :, :], xH[at]).then_inc(s["xL"], 1)

                def route(g):
                    link = Link(dve, s["own"], RL * g)
                    dve.wait_ge(s["logit"], g + 1)
                    wait(dve, s["score"], g)
                    wide = lambda v: v.unsqueeze(2).to_broadcast([P, GT, EXP])
                    nc.vector.tensor_reduce(top[:, :], pR[:, :, :], axis=AX.X, op=ALU.max).then_inc(s["top"], 1)
                    dve.wait_ge(s["top"], g + 1)
                    link(nc.vector.tensor_tensor(rank[:, :, :], pR[:, :, :], wide(top[:, :]), ALU.is_equal))
                    link(nc.vector.tensor_tensor(rank[:, :, :], rank[:, :, :], desc[:, :].unsqueeze(1).to_broadcast([P, GT, EXP]), ALU.mult))
                    link(nc.vector.tensor_reduce(first_of[:, :], rank[:, :, :], axis=AX.X, op=ALU.max))
                    link(nc.vector.tensor_tensor(onehot[:, bass.ds(g * GT, GT), :], rank[:, :, :], wide(first_of[:, :]), ALU.is_equal))
                    assert link.n == RL

                def scale(g):
                    dve.wait_ge(s["score"], g + 1)
                    if not (isinstance(g, int) and g == 0):
                        dve.wait_ge(s["xs_out"], 16 * g)
                    for i in range(GT):
                        m = nc.vector.tensor_scalar(xo[:, i, :], x3[:, i, :], score[:, i:i + 1], None, ALU.mult)
                    m.then_inc(s["xs"], 1)
                for i in range(GT):
                    norm(0, i)
                    x_low(i, i)

                def body(g, first, last):
                    for i in range(IC):
                        n = IC * g + i
                        dve.wait_ge(s["sig"], n + 1)
                        nc.vector.tensor_tensor(sg[:, i % 2, :], sg[:, i % 2, :], pG[i % 2][:, :], ALU.mult).then_inc(s["gated"], 1)
                        dve.wait_ge(s["gated"], n + 1)
                        dve.wait_ge(s["up"], n + 1)
                        wait(dve, s["hL"], n - 1)
                        nc.vector.tensor_tensor(h[:, i % 2, :], sg[:, i % 2, :], pU[i % 2][:, :], ALU.mult).then_inc(s["h"], 1)
                        if i == 0:
                            route(g)
                        if i == 2:
                            scale(g)
                        dve.wait_ge(s["hH"], n + 1)
                        sub(hL[:, i, :], h[:, i % 2, :], hH[:, i, :]).then_inc(s["hL"], 1)
                        if i == IC - 1 and not last:
                            dve.wait_ge(s["xs"], g + 1)
                            norm(g + 1, 0)
                    for i in range(GT):
                        if not last:
                            x_low(GT * g + GT + i, i)
                            if i < GT - 1:
                                norm(g + 1, i + 1)
                        t = GT * g + i
                        dve.wait_ge(s["down"], t + 1)
                        dve.wait_ge(s[f"r_in{i % 2}"], 16 * (g * (GT // 2) + i // 2 + 1))
                        wait(dve, s[f"out{i % 2}"], 16 * (g * (GT // 2) + i // 2))
                        nc.vector.tensor_tensor(o3[:, i % 2, :], pD[i % 2][:, :], xr[:, i % 2, :], ALU.add).then_inc(s["sum"], 1)
                groups(dve, body)

            @block.tensor
            def _(pe):
                def x_transpose(t, i):
                    pe.wait_ge(s["normed"], t + 1)
                    wait(pe, s["xL"], t)
                    for a in range(KC):
                        m = nc.tensor.transpose(pX[:, a, :], x3[:, i, a * P:(a + 1) * P], ident[:, :])
                    m.then_inc(s["xt"], 1)
                for i in range(GT):
                    x_transpose(i, i)

                def hidden(out, wH, wL, i, count):
                    for a in range(KC):
                        at = (slice(None), a, slice(i * P, (i + 1) * P))
                        m = split_matmuls(nc, out, (wH[at], wL[at]), (xH[:, a, :], xL[:, a, :]), a == 0, a == KC - 1)
                    m.then_inc(count, 1)

                def logits(g):
                    wait(pe, s["own"], RL * g)
                    for t in range(GT):
                        for a in range(KC):
                            at = (slice(None), a, slice(t * P, (t + 1) * P))
                            m = split_matmuls(nc, pR[:, t, :], (xH[at], xL[at]), (rH[:, a, :], rL[:, a, :]), a == 0, a == KC - 1)
                    m.then_inc(s["logit"], 1)

                def body(g, first, last):
                    pe.wait_ge(s["xL"], GT * g + GT)
                    for i in range(IC):
                        n = IC * g + i
                        wait(pe, s["h"], n - 1)
                        hidden(pG[i % 2][:, :], wgH, wgL, i, s["gate"])
                        hidden(pU[i % 2][:, :], wuH, wuL, i, s["up"])
                        if i == 0:
                            logits(g)
                    for i in range(GT):
                        t = GT * g + i
                        if not last:
                            x_transpose(t + GT, i)
                        wait(pe, s["sum"], t - 1)
                        for c in range(IC):
                            if i == 0:
                                pe.wait_ge(s["hL"], IC * g + c + 1)
                            at = (slice(None), c, slice(i * P, (i + 1) * P))
                            m = split_matmuls(nc, pD[i % 2][:, :], (hH[at], hL[at]), (wdH[:, c, :], wdL[:, c, :]), c == 0, c == IC - 1)
                        m.then_inc(s["down"], 1)
                groups(pe, body)


def routing_tables(nc, onehot, index, table, mybir, ExitStack):
    F32, BF, I32 = mybir.dt.float32, mybir.dt.bfloat16, mybir.dt.int32
    ALU, AX = mybir.AluOpType, mybir.AxisListType
    EXP = onehot.shape[2]
    NSLOT, NIDX = table.shape[2], index.shape[1]
    with ExitStack() as ctx:
        sb = lambda n, s, d=F32: ctx.enter_context(nc.sbuf_tensor("r_" + n, s, d))
        ps = lambda n, s: ctx.enter_context(nc.psum_tensor("r_" + n, s, F32))
        tri, ones = sb("tri", [P, P], BF), sb("ones", [P, P], BF)
        rampi, lanei = sb("rampi", [P, P], I32), sb("lanei", [P, 1], I32)
        ramp, lane, thr = sb("ramp", [P, P]), sb("lane", [P, 1]), sb("thr", [P, EXP - 1])
        A, B = sb("A", [P, TILES, EXP]), sb("B", [P, TILES, EXP])
        cmp_n, cmp_s = sb("cmp_n", [P, EXP, EXP - 1]), sb("cmp_s", [P, NSLOT + 1, EXP])
        n_e, ea, eb, st128 = sb("n_e", [P, EXP]), sb("ea", [P, EXP]), sb("eb", [P, EXP]), sb("st128", [P, EXP])
        pos, posr, posq = sb("pos", [P, TILES]), sb("posr", [P, TILES]), sb("posq", [P, TILES])
        pi, pt = sb("pi", [P, TILES], I32), sb("pt", [P, TILES], I32)
        inrow, inslot = sb("inrow", [P, TILES, P], BF), sb("inslot", [P, TILES, 3, NIDX], BF)
        e_of, act_f, idx_f = sb("e_of", [P, NSLOT + 1]), sb("act_f", [P, NSLOT]), sb("idx_f", [P, NIDX])
        pR, pT = ps("pR", [P, 2, TILES // 2, EXP]), ps("pT", [P, 2, TILES // 2, EXP])
        pI = ps("pI", [P, 3, NIDX])
        s = {n: ctx.enter_context(nc.semaphore("r_" + n)) for n in "ones tri rampi own counted placed indexed".split()}
        block = ctx.enter_context(nc.Block())

        @block.gpsimd
        def _(pool):
            nc.gpsimd.memset(ones[:, :], 1.0).then_inc(s["ones"], 1)
            nc.gpsimd.iota(rampi[:, :], pattern=[[1, P]], base=0, channel_multiplier=0).then_inc(s["rampi"], 1)
            nc.gpsimd.iota(lanei[:, :], pattern=[[0, 1]], base=0, channel_multiplier=1).then_inc(s["rampi"], 1)
            pool.wait_ge(s["ones"], 1)
            nc.gpsimd.affine_select(out=tri[:, :], in_=ones[:, :], compare_op=ALU.is_gt, fill=0.0,
                                    base=0, pattern=[[1, P]], channel_multiplier=-1).then_inc(s["tri"], 1)

        @block.tensor
        def _(pe):
            pe.wait_ge(s["tri"], 1)
            half = TILES // 2
            for i in range(2):
                nc.tensor.matmul(pR[:, i, :, :], tri[:, :], onehot[:, i * half:(i + 1) * half, :], start=True, stop=True)
            for i in range(2):
                m = nc.tensor.matmul(pT[:, i, :, :], ones[:, :], onehot[:, i * half:(i + 1) * half, :], start=True, stop=True)
            m.then_inc(s["counted"], 1)
            pe.wait_ge(s["placed"], 1)
            for t in range(TILES):
                m = nc.tensor.matmul(pI[:, :, :], inrow[:, t, :], inslot[:, t, :, :], start=t == 0, stop=t == TILES - 1)
            m.then_inc(s["indexed"], 1)

        @block.vector
        def _(dve):
            v = nc.vector
            link = Link(dve, s["own"])
            flat = lambda a: a.rearrange("p i t e -> p (i t) e")
            dve.wait_ge(s["rampi"], 2)
            link(v.tensor_copy(ramp[:, :], rampi[:, :]))
            link(v.tensor_copy(lane[:, :], lanei[:, :]))
            link(v.tensor_scalar(thr[:, :], ramp[:, 1:EXP], float(P), None, ALU.mult))
            dve.wait_ge(s["counted"], 1)
            link(v.tensor_copy(A[:, :, :], flat(pT[:, :, :, :])))

            def running(a, b, n, axis_len):
                d = 1
                while d < axis_len:
                    v.tensor_copy(b[:, 0:d], a[:, 0:d])
                    link(v.tensor_tensor(b[:, d:], a[:, d:], a[:, 0:axis_len - d], ALU.add))
                    a, b, d = b, a, 2 * d
                return a
            incl = running(A, B, TILES, TILES)
            link(v.tensor_tensor(cmp_n[:, :, :], incl[:, TILES - 1, :].unsqueeze(2).to_broadcast([P, EXP, EXP - 1]),
                                 thr[:, :].unsqueeze(1).to_broadcast([P, EXP, EXP - 1]), ALU.is_gt))
            link(v.tensor_reduce(n_e[:, :], cmp_n[:, :, :], axis=AX.X, op=ALU.add))
            link(v.tensor_scalar(n_e[:, :], n_e[:, :], 1.0, None, ALU.add))
            link(v.tensor_copy(ea[:, :], n_e[:, :]))
            end = running(ea, eb, EXP, EXP)
            link(v.tensor_tensor(st128[:, :], end[:, :], n_e[:, :], ALU.subtract))
            link(v.tensor_scalar(st128[:, :], st128[:, :], float(P), None, ALU.mult))
            other = B if incl is A else A
            link(v.tensor_tensor(other[:, :, :], incl[:, :, :], flat(pT[:, :, :, :]), ALU.subtract))
            link(v.tensor_tensor(other[:, :, :], other[:, :, :], flat(pR[:, :, :, :]), ALU.add))
            link(v.tensor_tensor(other[:, :, :], other[:, :, :], st128[:, :].unsqueeze(1).to_broadcast([P, TILES, EXP]), ALU.add))
            link(v.tensor_tensor(other[:, :, :], other[:, :, :], onehot[:, :, :], ALU.mult))
            link(v.tensor_reduce(pos[:, :], other[:, :, :], axis=AX.X, op=ALU.add))
            link(v.tensor_copy(pi[:, :], pos[:, :]))
            link(v.tensor_single_scalar(pt[:, :], pi[:, :], P - 1, op=ALU.bitwise_and))
            link(v.tensor_copy(posr[:, :], pt[:, :]))
            link(v.tensor_single_scalar(pi[:, :], pi[:, :], P.bit_length() - 1, op=ALU.logical_shift_right))
            link(v.tensor_copy(posq[:, :], pi[:, :]))
            link(v.tensor_tensor(inrow[:, :, :], posr[:, :].unsqueeze(2).to_broadcast([P, TILES, P]),
                                 ramp[:, :].unsqueeze(1).to_broadcast([P, TILES, P]), ALU.is_equal))
            link(v.tensor_tensor(inslot[:, :, 0, :], posq[:, :].unsqueeze(2).to_broadcast([P, TILES, NIDX]),
                                 ramp[:, 0:NIDX].unsqueeze(1).to_broadcast([P, TILES, NIDX]), ALU.is_equal))
            link(v.tensor_scalar(inslot[:, :, 1, :], inslot[:, :, 0, :], lane[:, 0:1], None, ALU.mult))
            link(v.tensor_tensor(inslot[:, :, 2, :], inslot[:, :, 0, :], ramp[:, 0:TILES].unsqueeze(2).to_broadcast([P, TILES, NIDX]), ALU.mult))
            v.tensor_copy(idx_f[:, :], ramp[:, 0:NIDX]).then_inc(s["placed"], 1)
            link(v.tensor_tensor(cmp_s[:, :, :], ramp[:, 0:NSLOT + 1].unsqueeze(2).to_broadcast([P, NSLOT + 1, EXP]),
                                 end[:, :].unsqueeze(1).to_broadcast([P, NSLOT + 1, EXP]), ALU.is_ge))
            link(v.tensor_reduce(e_of[:, :], cmp_s[:, :, :], axis=AX.X, op=ALU.add))
            link(v.tensor_copy(table[:, 1, :], e_of[0:1, 0:NSLOT]))
            link(v.tensor_tensor(act_f[:, :], e_of[:, 1:NSLOT + 1], e_of[:, 0:NSLOT], ALU.subtract))
            link(v.scalar_tensor_tensor(out=act_f[:, :], in0=e_of[:, 0:NSLOT], scalar=float(EXP - 1), in1=act_f[:, :],
                                        op0=ALU.is_lt, op1=ALU.mult))
            link(v.scalar_tensor_tensor(out=act_f[:, :], in0=e_of[:, 0:NSLOT], scalar=float(EXP), in1=act_f[:, :],
                                        op0=ALU.is_lt, op1=ALU.add))
            link(v.tensor_copy(table[:, 0, :], act_f[0:1, :]))
            dve.wait_ge(s["indexed"], 1)
            link(v.tensor_scalar(idx_f[:, :], pI[:, 0, :], -float(TOK), float(TOK), ALU.mult, ALU.add))
            link(v.tensor_tensor(idx_f[:, :], idx_f[:, :], pI[:, 1, :], ALU.add))
            link(v.scalar_tensor_tensor(out=idx_f[:, :], in0=pI[:, 2, :], scalar=float(P), in1=idx_f[:, :], op0=ALU.mult, op1=ALU.add))
            link(v.tensor_copy(index[:, :], idx_f[:, :]))


def routed_experts(nc, ident, xs, base, Wg, Wu, Wd, index, table, out, mybir, bass, ExitStack):
    F32, F32R, I32 = mybir.dt.float32, mybir.dt.float32r, mybir.dt.int32
    ALU, ACT = mybir.AluOpType, mybir.ActivationFunctionType
    EXP, _, IW = Wg.shape
    IC = IW // P
    HALF = IW // 2
    BLOCK = 8
    GU, DN = 2 * KC, IC // 2
    PIECES = GU + DN
    POOL_LOW = (1, 4, 6, 8)
    DVE_HIGH = (2, 8)
    NPL, NDL, NDH = len(POOL_LOW), PIECES - len(POOL_LOW), len(DVE_HIGH)
    NAH = PIECES - NDH
    with ExitStack() as ctx:
        sb = lambda n, s, d=F32: ctx.enter_context(nc.sbuf_tensor("d_" + n, s, d))
        ps = lambda n, s: ctx.enter_context(nc.psum_tensor("d_" + n, s, F32))
        raw = sb("raw", [P, PIECES, 2, HALF])
        wH, wL = (sb(n, [P, PIECES, 2, HALF], F32R) for n in ("wH", "wL"))
        xg, bg, og = sb("xg", [P, C]), sb("bg", [P, C]), sb("og", [P, C])
        ix, ib = sb("ix", [P, 1], I32), sb("ib", [P, 1], I32)
        xH, xL = (sb(n, [P, KC, P], F32R) for n in ("xH", "xL"))
        sg, h = sb("sg", [P, 2, HALF]), sb("h", [P, 2, HALF])
        hH, hL = (sb(n, [P, IC, P], F32R) for n in ("hH", "hL"))
        pG = [ps(f"pG{i}", [P, HALF]) for i in range(2)]
        pU = [ps(f"pU{i}", [P, HALF]) for i in range(2)]
        pT = [ps(f"pT{i}", [P, IC // 2, P]) for i in range(2)]
        pX, pD = ps("pX", [P, KC, P]), ps("pD", [P, C])
        names = ("zero ix ib x_in b_in turn xt xH xL silu h ht hH hL used sum"
                 " highA highD lowD lowP").split()
        s = {n: ctx.enter_context(nc.semaphore("d_" + n)) for n in names}
        win = [ctx.enter_context(nc.semaphore(f"d_w_in{n}")) for n in range(PIECES)]
        wsize = [32 if n < GU else 16 for n in range(PIECES)]

        def upto(members, n):
            return sum(1 for m in members if m <= n)
        DVE_LOW = tuple(n for n in range(PIECES) if n not in POOL_LOW)
        ACT_HIGH = tuple(n for n in range(PIECES) if n not in DVE_HIGH)

        def wait_high(eng, e, n):
            if n in DVE_HIGH:
                eng.wait_ge(s["highD"], NDH * e + upto(DVE_HIGH, n))
            else:
                eng.wait_ge(s["highA"], NAH * e + upto(ACT_HIGH, n))

        def wait_low(eng, e, n):
            if n in POOL_LOW:
                eng.wait_ge(s["lowP"], NPL * e + upto(POOL_LOW, n))
            else:
                eng.wait_ge(s["lowD"], NDL * e + upto(DVE_LOW, n))

        def wait_raw(eng, e, n):
            eng.wait_ge(win[n], wsize[n] * (e + 1))

        def high_piece(eng, e, n):
            wait_raw(eng, e, n)
            if n in DVE_HIGH:
                nc.vector.tensor_copy(wH[:, n, :, :], raw[:, n, :, :]).then_inc(s["highD"], 1)
            else:
                nc.scalar.copy(wH[:, n, :, :], raw[:, n, :, :]).then_inc(s["highA"], 1)

        def low_piece(eng, unit, e, n, count):
            wait_raw(eng, e, n)
            wait_high(eng, e, n)
            unit.tensor_tensor(wL[:, n, :, :], raw[:, n, :, :], wH[:, n, :, :].bitcast(F32), ALU.subtract).then_inc(count, 1)

        def slots(eng, body):
            look = lambda i, t, top: eng.value_load(table[0:1, i, bass.ds(t, 1)], min_val=0, max_val=top)
            with eng.Fori(0, table.shape[2] // BLOCK) as b:
                with eng.If(look(0, b * BLOCK, 2) > 0):
                    with eng.Fori(0, BLOCK) as i:
                        t = b * BLOCK + i
                        kind = look(0, t, 2)
                        with eng.If(kind == 1):
                            body(t, look(1, t, EXP), False)
                        with eng.If(kind == 2):
                            body(t, look(1, t, EXP), True)

        block = ctx.enter_context(nc.Block())

        @block.sync
        def _(sp):
            def load(e, n):
                one = lambda w: w[bass.ds(e, 1), :, :].rearrange("o (a p) n -> (o a) p n", p=P)
                if n < GU:
                    a, half = n % KC, slice(n // KC * HALF, (n // KC + 1) * HALF)
                    for i, w in enumerate((Wg, Wu)):
                        sp.dma_start(raw[:, n, i, :], one(w)[a, :, half]).then_inc(win[n], 16)
                else:
                    a = 2 * (n - GU)
                    sp.dma_start(raw[:, n, :, :], one(Wd)[a:a + 2, :, :].rearrange("a p n -> p a n")).then_inc(win[n], 16)
            for n in range(PIECES):
                load(0, n)
            with sp.Fori(1, EXP) as e:
                for n in range(PIECES):
                    wait_low(sp, e - 1, n)
                    load(e, n)

        @block.gpsimd
        def _(pool):
            indirect = bass.IndirectOffsetOnAxis
            bound = pool.to_reg(TOK - 1)
            for a in (xg, bg):
                nc.gpsimd.memset(a[:, :], 0.0).then_inc(s["zero"], 1)
            pool.wait_ge(s["zero"], 2)

            def indirect_dma(count, **how):
                pool.indirect_dma_start(bounds_check=bound, oob_is_err=False, **how).then_inc(count, 16)

            def gather_x(t, copied, count, arrived):
                nc.gpsimd.tensor_copy(ix[:, :], index[:, bass.ds(t, 1)]).then_inc(copied, 1)
                pool.wait_ge(s["zero"], 2)
                pool.wait_ge(copied, count)
                indirect_dma(arrived, out=xg[:, :], out_offset=None, in_=xs, in_offset=indirect(ap=ix[:, 0:1], axis=0))

            def low(e, n):
                low_piece(pool, nc.gpsimd, e, n, s["lowP"])
            gather_x(0, s["zero"], 3, s["turn"])
            pool.wait_ge(s["turn"], 16)
            pool.wait_ge(s["xt"], 1)
            gather_x(1, s["zero"], 4, s["x_in"])
            for n in POOL_LOW:
                low(0, n)

            def body(t, e, split):
                pool.wait_ge(s["turn"], 16 * t + 16)
                pool.wait_ge(s["xt"], t + 1)
                nc.gpsimd.tensor_copy(ib[:, :], index[:, bass.ds(t, 1)]).then_inc(s["ib"], 1)
                pool.wait_ge(s["zero"], 2)
                pool.wait_ge(s["ib"], t + 1)
                indirect_dma(s["b_in"], out=bg[:, :], out_offset=None, in_=base, in_offset=indirect(ap=ib[:, 0:1], axis=0))
                for n in POOL_LOW:
                    if split:
                        pool.wait_ge(s["used"], PIECES * t + n + 1)
                        low(e + 1, n)
                    if n == KC + 2:
                        pool.wait_ge(s["x_in"], 16 * t + 16)
                        pool.wait_ge(s["xt"], t + 2)
                        gather_x(t + 2, s["ix"], t + 1, s["x_in"])
                pool.wait_ge(s["zero"], 2)
                pool.wait_ge(s["b_in"], 16 * t + 16)
                pool.wait_ge(s["sum"], t + 1)
                indirect_dma(s["turn"], out=out, out_offset=indirect(ap=ib[:, 0:1], axis=0), in_=og[:, :], in_offset=None)
            slots(pool, body)

        @block.scalar
        def _(act):
            def x_high(t):
                act.wait_ge(s["xt"], t + 1)
                nc.scalar.copy(xH[:, :, :], pX[:, :, :]).then_inc(s["xH"], 1)
            x_high(0)
            for n in ACT_HIGH:
                high_piece(act, 0, n)

            def body(t, e, split):
                def high(*pieces):
                    for n in pieces:
                        if split and n in ACT_HIGH:
                            act.wait_ge(s["used"], PIECES * t + n + 1)
                            high_piece(act, e + 1, n)

                def silu(n):
                    act.wait_ge(s["used"], PIECES * t + KC * (n + 1))
                    nc.scalar.activation(sg[:, n, :], pG[n][:, :], ACT.Silu).then_inc(s["silu"], 1)

                def h_high(n):
                    act.wait_ge(s["ht"], 2 * t + n + 1)
                    nc.scalar.copy(hH[:, 4 * n:4 * n + 4, :], pT[n][:, :, :]).then_inc(s["hH"], 1)
                high(0, 1, 2)
                silu(0)
                high(3, 4)
                h_high(0)
                high(5, 6)
                silu(1)
                x_high(t + 1)
                h_high(1)
                high(7, 8, 9, 10, 11)
            slots(act, body)

        @block.vector
        def _(dve):
            sub = lambda out, in_, hi: nc.vector.tensor_tensor(out, in_, hi.bitcast(F32), ALU.subtract)

            def x_low(t):
                dve.wait_ge(s["xH"], t + 1)
                sub(xL[:, :, :], pX[:, :, :], xH[:, :, :]).then_inc(s["xL"], 1)
            x_low(0)
            for n in range(2):
                nc.vector.memset(h[:, n, :], 0.0).then_inc(s["h"], 1)
            for n in range(PIECES):
                if n in DVE_HIGH:
                    high_piece(dve, 0, n)
                if n in DVE_LOW:
                    low_piece(dve, nc.vector, 0, n, s["lowD"])

            def body(t, e, split):
                def low(*pieces):
                    for n in pieces:
                        if split:
                            if n in DVE_HIGH or n in DVE_LOW:
                                dve.wait_ge(s["used"], PIECES * t + n + 1)
                            if n in DVE_HIGH:
                                high_piece(dve, e + 1, n)
                            if n in DVE_LOW:
                                low_piece(dve, nc.vector, e + 1, n, s["lowD"])

                def gate(n):
                    dve.wait_ge(s["silu"], 2 * t + n + 1)
                    dve.wait_ge(s["h"], 2 * t + 2)
                    nc.vector.tensor_tensor(h[:, n, :], sg[:, n, :], pU[n][:, :], ALU.mult).then_inc(s["h"], 1)

                def h_low(n):
                    dve.wait_ge(s["hH"], 2 * t + n + 1)
                    sub(hL[:, 4 * n:4 * n + 4, :], pT[n][:, :, :], hH[:, 4 * n:4 * n + 4, :]).then_inc(s["hL"], 1)
                low(0, 1, 2)
                gate(0)
                low(3, 4)
                h_low(0)
                low(5, 6)
                gate(1)
                x_low(t + 1)
                h_low(1)
                low(7, 8, 9, 10, 11)
                dve.wait_ge(s["used"], PIECES * (t + 1))
                dve.wait_ge(s["b_in"], 16 * t + 16)
                nc.vector.tensor_tensor(og[:, :], pD[:, :], bg[:, :], ALU.add).then_inc(s["sum"], 1)
            slots(dve, body)

        @block.tensor
        def _(pe):
            def x_transpose(arrived, count):
                pe.wait_ge(arrived, count)
                for a in range(KC):
                    m = nc.tensor.transpose(pX[:, a, :], xg[:, a * P:(a + 1) * P], ident[:, :])
                m.then_inc(s["xt"], 1)
            x_transpose(s["turn"], 16)

            def body(t, e, split):
                def gate_up(half, chunks):
                    for a in chunks:
                        n = half * KC + a
                        wait_low(pe, e, n)
                        for i, (x, w, first, last) in enumerate(((xH, wH, a == 0, False), (xH, wL, False, False), (xL, wH, False, a == KC - 1))):
                            for j, bank in enumerate((pG, pU)):
                                m = nc.tensor.matmul(bank[half][:, :], x[:, a, :], w[:, n, j, :], start=first, stop=last)
                        m.then_inc(s["used"], 1)

                def h_transpose(half):
                    pe.wait_ge(s["h"], 2 * t + 2 + half + 1)
                    for c in range(IC // 2):
                        m = nc.tensor.transpose(pT[half][:, c, :], h[:, half, c * P:(c + 1) * P], ident[:, :])
                    m.then_inc(s["ht"], 1)

                def down(n):
                    wait_low(pe, e, n)
                    pe.wait_ge(s["hL"], 2 * t + (n - GU) // (DN // 2) + 1)
                    for i in range(2):
                        c = 2 * (n - GU) + i
                        m = split_matmuls(nc, pD[:, :], (hH[:, c, :], hL[:, c, :]), (wH[:, n, i, :], wL[:, n, i, :]), c == 0, c == IC - 1)
                    return m.then_inc(s["used"], 1)
                pe.wait_ge(s["xL"], t + 1)
                pe.wait_ge(s["h"], 2 * t + 2)
                gate_up(0, range(KC))
                gate_up(1, range(KC // 2))
                h_transpose(0)
                gate_up(1, range(KC // 2, KC))
                x_transpose(s["x_in"], 16 * t + 16)
                pe.wait_ge(s["b_in"], 16 * t + 16)
                down(GU)
                h_transpose(1)
                for n in range(GU + 1, PIECES):
                    down(n)
            slots(pe, body)


def decoder_layer(nc, x, ctx_in, mask, w_fc, w_proj, ln_g, ln_b, Wq, Wk, Wv, Wo, gate_w, sg_w, su_w, sd_w, rg_w, ru_w, rd_w, out):
    F32 = mybir.dt.float32
    x1, x2, xs, base = (nc.dram_tensor(n, (TOK, C), F32, kind="Internal").ap() for n in ("x1", "x2", "xs", "base"))
    slots = 2 * (TOK // P)
    experts = gate_w.shape[1]
    ident_ctx = ExitStack()
    ident = ident_ctx.enter_context(nc.sbuf_tensor("ident", [P, P], F32))
    stats = ident_ctx.enter_context(nc.sbuf_tensor("stats", [P, TILES, KC, 6], F32))
    self_attention(nc, ident, stats, x, w_fc, w_proj, ln_g, ln_b, x1, mybir, bass, ExitStack)
    cross_attention(nc, ident, stats, x1, ctx_in, mask, Wq, Wk, Wv, Wo, x2, mybir, bass, ExitStack)
    with ExitStack() as ctx:
        onehot = ctx.enter_context(nc.sbuf_tensor("onehot", [P, TILES, experts], mybir.dt.bfloat16))
        index = ctx.enter_context(nc.sbuf_tensor("index", [P, slots + 2], mybir.dt.int32))
        table = ctx.enter_context(nc.sbuf_tensor("table", [1, 2, slots], mybir.dt.int32))
        shared_experts(nc, ident, stats, x2, gate_w, sg_w, su_w, sd_w, onehot, xs, base, mybir, bass, ExitStack)
        routing_tables(nc, onehot, index, table, mybir, ExitStack)
        routed_experts(nc, ident, xs, base, rg_w, ru_w, rd_w, index, table, out, mybir, bass, ExitStack)
    ident_ctx.close()


_INS = ["x", "ctx_1024", "mask_SxS2_bk0", "L0_attn_w_fc", "L0_attn_w_proj", "L0_attn_ln_g", "L0_attn_ln_b",
        "L0_xattn_Wq", "L0_xattn_Wk", "L0_xattn_Wv", "L0_xattn_Wo", "L0_ffn_gate_w", "L0_ffn_shared_gate_w",
        "L0_ffn_shared_up_w", "L0_ffn_shared_down_w", "L0_ffn_routed_gate_w", "L0_ffn_routed_up_w", "L0_ffn_routed_down_w"]


def kernel(**inputs):
    import numpy as np
    import concourse.bacc as bacc
    from concourse.bass_utils import run_bass_kernel_spmd

    nc = bacc.Bacc("TRN2", target_bir_lowering=False, num_devices=1)
    arrays, args = {}, []
    for name in _INS:
        a = np.ascontiguousarray(inputs[name])
        if name == "x":
            a = a.reshape(TOK, C)
        arrays[f"in_{name}"] = a
        args.append(nc.dram_tensor(f"in_{name}", a.shape, mybir.dt.from_np(a.dtype), kind="ExternalInput").ap())
    out = nc.dram_tensor("out_0", (TOK, C), mybir.dt.float32, kind="ExternalOutput").ap()
    decoder_layer(nc, *args, out)
    r = run_bass_kernel_spmd(nc, [arrays], core_ids=[0])
    return r.results[0]["out_0"].reshape(NB, TOK // NB, C)
```

```python
from contextlib import ExitStack

import concourse.bass as bass
from concourse import mybir

TOK, C, P = 4096, 512, 128
NB = 2
KC = C // P
TILES = TOK // P
GT = 4
GTOK = GT * P
GROUPS = TOK // GTOK
EPS = 1e-5


class Link:

    def __init__(self, eng, sem, base=0):
        self.eng, self.sem, self.base, self.n = eng, sem, base, 0

    def __call__(self, ins):
        self.n += 1
        ins.then_inc(self.sem, 1)
        self.eng.wait_ge(self.sem, self.base + self.n)


def rsqrt(nc, link, y, t, v, ALU, I32):
    link(nc.vector.tensor_single_scalar(t.bitcast(I32), v.bitcast(I32), 1, op=ALU.logical_shift_right))
    link(nc.vector.tensor_scalar(y.bitcast(I32), t.bitcast(I32), -1.0, float(0x5F3759DF), ALU.mult, ALU.add))
    for _ in range(4):
        link(nc.vector.scalar_tensor_tensor(out=t, in0=y, scalar=-0.5, in1=y, op0=ALU.mult, op1=ALU.mult))
        link(nc.vector.tensor_tensor(t, t, v, ALU.mult))
        link(nc.vector.scalar_tensor_tensor(out=y, in0=t, scalar=1.5, in1=y, op0=ALU.add, op1=ALU.mult))


def split_matmuls(nc, out, a, b, first, last):
    nc.tensor.matmul(out, a[0], b[0], start=first, stop=False)
    nc.tensor.matmul(out, a[0], b[1], start=False, stop=False)
    return nc.tensor.matmul(out, a[1], b[0], start=False, stop=last)


def self_attention(nc, ident, stats, x, w_fc, w_proj, ln_g, ln_b, x1, mybir, bass, ExitStack):
    F32, F32R, I32 = mybir.dt.float32, mybir.dt.float32r, mybir.dt.int32
    ALU, ACT = mybir.AluOpType, mybir.ActivationFunctionType
    NH = C // P
    S = C * C // P
    SC = S // P
    NPAIR = SC // 2
    POOL_LOW = (1, 4, 6)
    NPL = len(POOL_LOW)
    x_t = x.rearrange("(t p) c -> p t c", p=P)
    x1_t = x1.rearrange("(t p) c -> p t c", p=P)
    with ExitStack() as ctx:
        sb = lambda n, s, d=F32: ctx.enter_context(nc.sbuf_tensor("a_" + n, s, d))
        ps = lambda n, s: ctx.enter_context(nc.psum_tensor("a_" + n, s, F32))
        sem = lambda n: ctx.enter_context(nc.semaphore("a_" + n))
        kH, kL = (sb(n, [P, SC, P], F32R) for n in ("kH", "kL"))
        vH, vL = (sb(n, [P, SC, P], F32R) for n in ("vH", "vL"))
        qH, qL = (sb(n, [P, 2, NH, GTOK], F32R) for n in ("qH", "qL"))
        base = sb("base", [P, 2, GT, C])
        gB, bB = sb("gB", [P, C]), sb("bB", [P, C])
        wf, wp = sb("wf", [P, KC, C]), sb("wp", [P, KC, C])
        xg = sb("xg", [P, 2, GT, C])
        st, mv = sb("st", [P, TILES, 6]), sb("mv", [P, TILES, 2])
        v1, v2, r1, r2, tmp = (sb(n, [P, TILES]) for n in ("v1", "v2", "r1", "r2", "tmp"))
        xb, y, qn = sb("xb", [P, 2, C]), sb("y", [P, C]), sb("qn", [P, C])
        r, p = sb("r", [P, 2, 2, GTOK]), sb("p", [P, 2, 2, GTOK])
        pH, pL = (sb(n, [P, 4, 2, GTOK], F32R) for n in ("pH", "pL"))
        oT, o1 = sb("oT", [P, GTOK]), sb("o1", [P, 2, GT, P])
        pS = [ps(f"pS{i}", [P, 2, GTOK]) for i in range(2)]
        pO = [ps(f"pO{i}", [P, GTOK]) for i in range(2)]
        pX, pT = ps("pX", [P, NH, P]), ps("pT", [P, GT, P])
        kv = [pS[i][:, 0, :] for i in range(2)]

        names = ("ident0 ident w_in gb_in stat_in0 stat_in1 stat own_dve own_pool kv_t kvH kvL x_in0 x_in1 prep affined based"
                 " xt qH qL score relu pH p lowD lowP pv oT ot o1 out0 out1").split()
        s = {n: sem(n) for n in names}

        def pools(k, c):
            return NPL * k + sum(1 for m in POOL_LOW if m <= c)

        def dves(k, c):
            return (NPAIR - NPL) * k + sum(1 for m in range(c + 1) if m not in POOL_LOW)

        def wait_low(eng, k, c):
            if c < 0:
                k, c = k - 1, c + NPAIR
            if c in POOL_LOW:
                eng.wait_ge(s["lowP"], pools(k, c))
            else:
                eng.wait_ge(s["lowD"], dves(k, c))

        def groups(eng, body):
            body(0, True, False)
            with eng.Fori(1, GROUPS - 1) as g:
                body(g, False, False)
            body(GROUPS - 1, False, True)

        block = ctx.enter_context(nc.Block())

        @block.sync
        def _(sp):
            def load_rows(g):
                if g >= 2:
                    sp.wait_ge(s["stat"], GT * (g - 1))
                sp.dma_start(xg[:, g % 2, :, :], x_t[:, g * GT:(g + 1) * GT, :]).then_inc(s[f"stat_in{g % 2}"], 16)
            load_rows(0)
            load_rows(1)
            sp.dma_start(wf[:, :, :], w_fc.rearrange("(a p) c -> p a c", p=P)).then_inc(s["w_in"], 16)
            sp.dma_start(wp[:, :, :], w_proj.rearrange("(a p) c -> p a c", p=P)).then_inc(s["w_in"], 16)
            for row, tile in ((ln_g, gB), (ln_b, bB)):
                sp.dma_start(tile[:, :], row.rearrange("(o c) -> o c", o=1).to_broadcast([P, C])).then_inc(s["gb_in"], 16)

            def load(t, slot):
                sp.dma_start(xb[:, slot, :], x_t[:, bass.ds(t, 1), :].rearrange("p o c -> p (o c)")).then_inc(s[f"x_in{slot}"], 16)
            for t in range(GT):
                if t >= 2:
                    sp.wait_ge(s["based"], t - 1)
                load(t, t % 2)
            load_rows(2)
            load_rows(3)

            def body(g, first, last):
                for h in range(NH):
                    k = g * NH + h
                    if not last:
                        sp.wait_ge(s["based"], k + GT - 1)
                        load(k + GT, h % 2)
                    if first and 2 * h + 3 in range(5, GROUPS):
                        load_rows(2 * h + 3)
                    if not (first and h == 0):
                        sp.wait_ge(s["o1"], k)
                        store(g if h else g - 1, (h - 1) % NH)
                    if first and 2 * h + 4 < GROUPS:
                        load_rows(2 * h + 4)

            def store(g, h):
                sp.dma_start(x1_t[:, bass.ds(g * GT, GT), h * P:(h + 1) * P], o1[:, h % 2, :, :]).then_inc(s[f"out{h % 2}"], 16)
            groups(sp, body)
            sp.wait_ge(s["o1"], GROUPS * NH)
            store(GROUPS - 1, NH - 1)
            for slot in range(2):
                sp.wait_ge(s[f"out{slot}"], 16 * GROUPS * NH // 2)

        @block.gpsimd
        def _(pool):
            nc.gpsimd.memset(ident[:, :], 0.0).then_inc(s["ident0"], 1)
            pool.wait_ge(s["ident0"], 1)
            nc.gpsimd.affine_select(out=ident[:, :], in_=ident[:, :], compare_op=ALU.not_equal, fill=1.0,
                                    base=0, pattern=[[-1, P]], channel_multiplier=1).then_inc(s["ident"], 1)
            pool.wait_ge(s["gb_in"], 32)

            def affine(t, link):
                pool.wait_ge(s["prep"], 2 * t + 2)
                link(nc.gpsimd.tensor_tensor(qn[:, :], qn[:, :], gB[:, :], ALU.mult))
                nc.gpsimd.tensor_tensor(qn[:, :], qn[:, :], bB[:, :], ALU.add).then_inc(s["affined"], 1)

            def add_base(g, t, h):
                nc.gpsimd.tensor_tensor(base[:, bass.ds(g % 2, 1), h, :].rearrange("p o c -> p (o c)"),
                                        xb[:, h % 2, :], y[:, :], ALU.add).then_inc(s["based"], 1)

            def low(k, c):
                pool.wait_ge(s["pH"], NPAIR * k + c + 1)
                pool.wait_ge(s["p"], NPAIR * k + c + 1)
                nc.gpsimd.tensor_tensor(pL[:, c % 4, :, :], p[:, c % 2, :, :], pH[:, c % 4, :, :].bitcast(F32),
                                        ALU.subtract).then_inc(s["lowP"], 1)
            for t in range(GT):
                pool.wait_ge(s["prep"], 2 * t + 2)
                add_base(0, t, t)

            def body(g, first, last):
                for h in range(NH):
                    k = g * NH + h
                    low(k, 1)
                    if not last:
                        affine(k + GT, Link(pool, s["own_pool"], k))
                    low(k, 4)
                    if not last:
                        if not first:
                            pool.wait_ge(s["o1"], g * NH)
                        add_base(g + 1, k + GT, h)
                    low(k, 6)
            groups(pool, body)

        @block.scalar
        def _(act):
            def high(out, in_, func=ACT.Copy):
                return nc.scalar.activation(out, in_, func)
            for n in range(2 * KC):
                act.wait_ge(s["kv_t"], n + 1)
                dst = (kH, vH)[n // KC]
                high(dst[:, (n % KC) * KC:(n % KC + 1) * KC, :], kv[n % 2].rearrange("p (a c) -> p a c", a=KC)).then_inc(s["kvH"], 1)

            def q_high(g, t, h):
                act.wait_ge(s["xt"], t + 1)
                high(qH[:, bass.ds(g % 2, 1), :, h * P:(h + 1) * P].rearrange("p o h c -> p (o h) c"),
                     pX[:, :, :]).then_inc(s["qH"], 1)
            for t in range(GT):
                q_high(0, t, t)

            def out_copy(k, h):
                act.wait_ge(s["pv"], NPAIR * (k + 1))
                act.wait_ge(s["ot"], k) if not (isinstance(k, int) and k == 0) else None
                high(oT[:, :], pO[h % 2][:, :]).then_inc(s["oT"], 1)

            def body(g, first, last):
                for h in range(NH):
                    k = g * NH + h
                    for c in range(NPAIR):
                        n = NPAIR * k + c
                        early = first and h == 0
                        act.wait_ge(s["score"], n + 1)
                        if not (early and c < 2):
                            act.wait_ge(s["p"], n - 1)
                        high(r[:, c % 2, :, :], pS[c % 2][:, :, :], ACT.Relu).then_inc(s["relu"], 1)
                        act.wait_ge(s["relu"], n + 1)
                        if not (early and c < 4):
                            act.wait_ge(s["pv"], n - 3)
                        high(pH[:, c % 4, :, :], r[:, c % 2, :, :], ACT.Square).then_inc(s["pH"], 1)
                        if c == 2 and not early:
                            out_copy(k - 1, (h - 1) % NH)
                        if c == 6 and not last:
                            q_high(g + 1, k + GT, h)
            groups(act, body)
            out_copy(GROUPS * NH - 1, NH - 1)

        @block.vector
        def _(dve):
            link = Link(dve, s["own_dve"])

            def row_stats(t):
                dve.wait_ge(s[f"stat_in{t // GT % 2}"], 16 * (t // GT // 2 + 1))
                nc.vector.bn_stats(out=st[:, t, :], in_=xg[:, t // GT % 2, t % GT, :]).then_inc(s["stat"], 1)

            def scales(lo, up):
                dve.wait_ge(s["stat"], up)
                for t in range(lo, up):
                    m = nc.vector.bn_aggr(out=mv[:, t, :], in_=st[:, t, :])
                link(m)
                var, r1s, r2s, v1s, v2s, tmps = (a[:, lo:up] for a in (mv[:, :, 1], r1, r2, v1, v2, tmp))
                link(nc.vector.tensor_scalar(v1s, var, EPS, None, ALU.add))
                rsqrt(nc, link, r1s, tmps, v1s, ALU, I32)
                link(nc.vector.tensor_tensor(tmps, r1s, r1s, ALU.mult))
                link(nc.vector.tensor_tensor(tmps, tmps, var, ALU.mult))
                link(nc.vector.tensor_scalar(v2s, tmps, EPS, None, ALU.add))
                rsqrt(nc, link, r2s, tmps, v2s, ALU, I32)
                link(nc.vector.tensor_tensor(r2s, r2s, r1s, ALU.mult))
            for t in range(2 * GT):
                row_stats(t)
            scales(0, 2 * GT)
            for n in range(2 * KC):
                dve.wait_ge(s["kvH"], n + 1)
                high, low = ((kH, kL), (vH, vL))[n // KC]
                m = slice((n % KC) * KC, (n % KC + 1) * KC)
                nc.vector.tensor_tensor(low[:, m, :], kv[n % 2].rearrange("p (a c) -> p a c", a=KC),
                                        high[:, m, :].bitcast(F32), ALU.subtract).then_inc(s["kvL"], 1)

            def prep(g, h, first):
                t = g * GT + h
                at = bass.ds(t, 1)
                dve.wait_ge(s[f"x_in{h % 2}"], 16 * (g * (GT // 2) + h // 2 + 1))
                if not first:
                    dve.wait_ge(s["based"], t)
                    dve.wait_ge(s["xt"], t)
                mean = mv[:, at, 0]
                nc.vector.tensor_scalar(y[:, :], xb[:, h % 2, :], mean, r1[:, at], ALU.subtract, ALU.mult).then_inc(s["prep"], 1)
                nc.vector.tensor_scalar(qn[:, :], xb[:, h % 2, :], mean, r2[:, at], ALU.subtract, ALU.mult).then_inc(s["prep"], 1)

            def q_low(g, t, h):
                dve.wait_ge(s["qH"], t + 1)
                at = (bass.ds(g % 2, 1), slice(None), slice(h * P, (h + 1) * P))
                nc.vector.tensor_tensor(qL[(slice(None), *at)].rearrange("p o h c -> p (o h) c"), pX[:, :, :],
                                        qH[(slice(None), *at)].rearrange("p o h c -> p (o h) c").bitcast(F32),
                                        ALU.subtract).then_inc(s["qL"], 1)
            for t in range(GT):
                prep(0, t, t == 0)
                if t:
                    q_low(0, t - 1, t - 1)
                dve.wait_ge(s["prep"], 2 * t + 2)
                dve.wait_ge(s["gb_in"], 32)
                link(nc.vector.tensor_tensor(qn[:, :], qn[:, :], gB[:, :], ALU.mult))
                nc.vector.tensor_tensor(qn[:, :], qn[:, :], bB[:, :], ALU.add).then_inc(s["affined"], 1)
            q_low(0, GT - 1, GT - 1)

            def add_out(k, g, h, first):
                dve.wait_ge(s["ot"], k + 1)
                if not first:
                    dve.wait_ge(s[f"out{h % 2}"], 16 * (g * (NH // 2) + h // 2))
                nc.vector.tensor_tensor(o1[:, h % 2, :, :], pT[:, :, :],
                                        base[:, bass.ds(g % 2, 1), :, h * P:(h + 1) * P].rearrange("p o t c -> p (o t) c"),
                                        ALU.add).then_inc(s["o1"], 1)

            def out_stats(k, g, h):
                dve.wait_ge(s["o1"], k + 1)
                for i in range(GT):
                    nc.vector.bn_stats(out=stats[:, bass.ds(g * GT + i, 1), h, :].rearrange("p o s -> p (o s)"), in_=o1[:, h % 2, i, :])

            def body(g, first, last):
                for h in range(NH):
                    k = g * NH + h
                    for c in range(NPAIR):
                        n = NPAIR * k + c
                        early = first and h == 0
                        dve.wait_ge(s["relu"], n + 1)
                        if not (early and c < 2):
                            wait_low(dve, k, c - 2)
                        nc.vector.tensor_tensor(p[:, c % 2, :, :], r[:, c % 2, :, :], r[:, c % 2, :, :],
                                                ALU.mult).then_inc(s["p"], 1)
                        if c not in POOL_LOW:
                            dve.wait_ge(s["pH"], n + 1)
                            dve.wait_ge(s["p"], n + 1)
                            nc.vector.tensor_tensor(pL[:, c % 4, :, :], p[:, c % 2, :, :],
                                                    pH[:, c % 4, :, :].bitcast(F32), ALU.subtract).then_inc(s["lowD"], 1)
                        if c == 0 and not last:
                            prep(g + 1, h, False)
                        if first and 2 * GT + n < TILES:
                            row_stats(2 * GT + n)
                        if first and h == NH - 1 and c == 3:
                            scales(2 * GT, TILES)
                        if c == 5 and not early:
                            add_out(k - 1, g if h else g - 1, (h - 1) % NH, first and h <= 2)
                        if c == 7 and not early:
                            out_stats(k - 1, g if h else g - 1, (h - 1) % NH)
                        if c == 6 and not last:
                            q_low(g + 1, k + GT, h)
            groups(dve, body)
            add_out(GROUPS * NH - 1, GROUPS - 1, NH - 1, False)
            out_stats(GROUPS * NH - 1, GROUPS - 1, NH - 1)

        @block.tensor
        def _(pe):
            pe.wait_ge(s["ident"], 1)
            pe.wait_ge(s["w_in"], 32)
            for n in range(2 * KC):
                if n >= 2:
                    pe.wait_ge(s["kvL"], n - 1)
                for cb in range(KC):
                    j = n % KC
                    src = wf[:, cb, j * P:(j + 1) * P] if n < KC else wp[:, j, cb * P:(cb + 1) * P]
                    t = nc.tensor.transpose(kv[n % 2][:, cb * P:(cb + 1) * P], src, ident[:, :])
                t.then_inc(s["kv_t"], 1)

            def x_transpose(t, first):
                pe.wait_ge(s["affined"], t + 1)
                if not first:
                    pe.wait_ge(s["qL"], t)
                for h in range(NH):
                    m = nc.tensor.transpose(pX[:, h, :], qn[:, h * P:(h + 1) * P], ident[:, :])
                m.then_inc(s["xt"], 1)
            for t in range(GT):
                x_transpose(t, t == 0)
            pe.wait_ge(s["kvL"], 2 * KC)

            def products(k, h, c):
                n = NPAIR * k + c
                pe.wait_ge(s["pH"], n + 1)
                wait_low(pe, k, c)
                for i in range(2):
                    m = 2 * c + i
                    last = split_matmuls(nc, pO[h % 2][:, :], (vH[:, m, :], vL[:, m, :]),
                                         (pH[:, c % 4, i, :], pL[:, c % 4, i, :]), m == 0, m == SC - 1)
                last.then_inc(s["pv"], 1)

            def out_transpose(k, first):
                pe.wait_ge(s["oT"], k + 1)
                if not first:
                    pe.wait_ge(s["o1"], k)
                for t in range(GT):
                    m = nc.tensor.transpose(pT[:, t, :], oT[:, t * P:(t + 1) * P], ident[:, :])
                m.then_inc(s["ot"], 1)

            def body(g, first, last):
                pe.wait_ge(s["qL"], GT * g + GT)
                for h in range(NH):
                    k = g * NH + h
                    for c in range(NPAIR):
                        n = NPAIR * k + c
                        early = first and h == 0
                        if not (early and c < 2):
                            pe.wait_ge(s["relu"], n - 1)
                        for i in range(2):
                            m = 2 * c + i
                            at = (bass.ds(g % 2, 1), h, slice(None))
                            last_m = split_matmuls(nc, pS[c % 2][:, i, :], (kH[:, m, :], kL[:, m, :]),
                                                   tuple(q[(slice(None), *at)].rearrange("p o c -> p (o c)") for q in (qH, qL)),
                                                   True, True)
                        last_m.then_inc(s["score"], 1)
                        if c >= 2:
                            if c == 2 and not (first and h < 2):
                                pe.wait_ge(s["oT"], k - 1)
                            products(k, h, c - 2)
                        elif not early:
                            products(k - 1, h - 1, c + NPAIR - 2)
                        if c == 4 and not early:
                            out_transpose(k - 1, first and h == 1)
                        if c == 5 and not last:
                            x_transpose(k + GT, False)
            groups(pe, body)
            for c in (NPAIR - 2, NPAIR - 1):
                products(GROUPS * NH - 1, NH - 1, c)
            out_transpose(GROUPS * NH - 1, False)


def wait(eng, sem, value):
    if not (isinstance(value, int) and value <= 0):
        eng.wait_ge(sem, value)


def split_weights(nc, ctx, tag, parts, mybir):
    F32 = mybir.dt.float32
    SLOTS = 3
    stage = ctx.enter_context(nc.sbuf_tensor(tag + "stage", [128, SLOTS, 1024], F32))
    arrived = [ctx.enter_context(nc.semaphore(f"{tag}w_in{i}")) for i in range(SLOTS)]
    high_done = ctx.enter_context(nc.semaphore(tag + "w_high"))
    low_done = ctx.enter_context(nc.semaphore(tag + "w_low"))

    def shaped(ap, like):
        return ap.rearrange("p (a b) -> p a b", b=like.shape[-1]) if len(like.shape) == 3 else ap

    def load(sp, start=0, stop=len(parts)):
        for n in range(start, stop):
            src = parts[n][0]
            wait(sp, low_done, n + 1 - SLOTS)
            sp.dma_start(shaped(stage[:, n % SLOTS, :], src), src).then_inc(arrived[n % SLOTS], 16)

    def high(act, start=0, stop=len(parts)):
        for n in range(start, stop):
            src, hi, _ = parts[n]
            act.wait_ge(arrived[n % SLOTS], 16 * (n // SLOTS + 1))
            nc.scalar.activation(hi, shaped(stage[:, n % SLOTS, :], hi), mybir.ActivationFunctionType.Copy).then_inc(high_done, 1)

    def low(dve, start=0, stop=len(parts)):
        for n in range(start, stop):
            src, hi, lo = parts[n]
            dve.wait_ge(high_done, n + 1)
            nc.vector.tensor_tensor(lo, shaped(stage[:, n % SLOTS, :], lo), hi.bitcast(F32),
                                    mybir.AluOpType.subtract).then_inc(low_done, 1)
    return load, high, low, low_done


def layernorm_stats(nc, link, stats, parts, mv, var, tmp, rstd, mybir):
    ALU = mybir.AluOpType
    n = stats.shape[1]
    for t in range(n):
        m = nc.vector.bn_aggr(out=mv[:, t, :], in_=stats[:, t, 0:parts, :])
    link(m)
    link(nc.vector.tensor_scalar(var[:, :], mv[:, :, 1], EPS, None, ALU.add))
    rsqrt(nc, link, rstd[:, :], tmp[:, :], var[:, :], ALU, mybir.dt.int32)


def cross_attention(nc, ident, stats, x1, ctx_in, mask, Wq, Wk, Wv, Wo, x2, mybir, bass, ExitStack):
    F32, F32R, U8 = mybir.dt.float32, mybir.dt.float32r, mybir.dt.uint8
    ALU, ACT, AX = mybir.AluOpType, mybir.ActivationFunctionType, mybir.AxisListType
    HD = 64
    INNER = Wq.shape[1]
    NPAIR = INNER // P
    KEYS = ctx_in.shape[1]
    SCALE = HD ** -0.5
    FMAX = 3.4028234663852886e38
    ROWT = mask.shape[0] // P
    BG = GROUPS // NB
    SUB = 2 * GT
    EARLY = 2
    x1_t = x1.rearrange("(t p) c -> p t c", p=P)
    x2_t = x2.rearrange("(t p) c -> p t c", p=P)
    with ExitStack() as keep:
        sbk = lambda n, s, d=F32: keep.enter_context(nc.sbuf_tensor("b_" + n, s, d))
        kH, kL = (sbk(n, [P, NPAIR, 2, KEYS], F32R) for n in ("kH", "kL"))
        later = [nc.dram_tensor(f"later{n}", (P, NPAIR, KEYS), F32, kind="Internal").ap() for n in "HL"]
        vH, vL = (sbk(n, [KEYS, NB, NPAIR, 2, P], F32R) for n in ("vH", "vL"))
        wqH, wqL = (sbk(n, [P, KC, INNER], F32R) for n in ("wqH", "wqL"))
        woH, woL = (sbk(n, [P, NPAIR, C], F32R) for n in ("woH", "woL"))

        with ExitStack() as ctx:
            sb = lambda n, s, d=F32: ctx.enter_context(nc.sbuf_tensor("b_" + n, s, d))
            ps = lambda n, s: ctx.enter_context(nc.psum_tensor("b_" + n, s, F32))
            wkH, wkL = (sb(n, [P, KC, INNER], F32R) for n in ("wkH", "wkL"))
            wvH, wvL = (sb(n, [P, KC, INNER], F32R) for n in ("wvH", "wvL"))
            cx = sb("cx", [KEYS, NB, C])
            cH, cL = (sb(n, [P, KC, NB, KEYS], F32R) for n in ("cH", "cL"))
            k1 = [sb(n, [P, 2, KEYS], F32R) for n in ("k1H", "k1L")]
            pC = [ps(f"pC{i}", [P, 2, NB, KEYS]) for i in range(2)]
            pK = [ps(f"pK{i}", [P, NB, KEYS]) for i in range(2)]
            pV = [ps(f"pV{i}", [KEYS, NPAIR // 2, 2, HD]) for i in range(2)]
            s = {n: ctx.enter_context(nc.semaphore("bs_" + n)) for n in
                 "c_in zero ct cH cL k_ps kH kL k_out0 k_out1 v_ps vH vL".split()}
            parts = []
            for w, hi, lo in ((Wk, wkH, wkL), (Wv, wvH, wvL), (Wq, wqH, wqL)):
                w_v = w.rearrange("(a p) n -> p a n", p=P)
                parts += [(w_v[:, a, :], hi[:, a, :], lo[:, a, :]) for a in range(KC)]
            wo_v = Wo.rearrange("(a p) n -> p a n", p=P)
            parts += [(wo_v[:, a:a + 2, :], woH[:, a:a + 2, :], woL[:, a:a + 2, :]) for a in range(0, NPAIR, 2)]
            load, high, low, low_done = split_weights(nc, ctx, "bs_", parts, mybir)
            block = ctx.enter_context(nc.Block())

            @block.sync
            def _(sp):
                sp.dma_start(cx[:, :, :], ctx_in.rearrange("b k c -> k b c")).then_inc(s["c_in"], 16)
                load(sp)

            @block.gpsimd
            def _(pool):
                nc.gpsimd.memset(kH[:, :, :, :].bitcast(F32), 0.0).then_inc(s["zero"], 1)
                nc.gpsimd.memset(kL[:, :, :, :].bitcast(F32), 0.0).then_inc(s["zero"], 1)
                nc.gpsimd.memset(vH[:, :, :, :, :].bitcast(F32), 0.0).then_inc(s["zero"], 1)
                nc.gpsimd.memset(vL[:, :, :, :, :].bitcast(F32), 0.0).then_inc(s["zero"], 1)
                for j in range(NPAIR):
                    pool.wait_ge(s["kL"], j + 1)
                    for part, dst in zip(k1, later):
                        pool.dma_start(dst[:, j, :], part[:, j % 2, :].bitcast(F32)).then_inc(s[f"k_out{j % 2}"], 16)
                for i in range(2):
                    pool.wait_ge(s[f"k_out{i}"], 32 * NPAIR // 2)

            @block.scalar
            def _(act):
                copy = lambda out, in_: nc.scalar.activation(out, in_, ACT.Copy)
                for i in range(2):
                    act.wait_ge(s["ct"], i + 1)
                    copy(cH[:, 2 * i:2 * i + 2, :, :], pC[i][:, :, :, :]).then_inc(s["cH"], 1)
                high(act, 0, KC)
                act.wait_ge(s["zero"], 2)
                for j in range(NPAIR):
                    high(act, KC + j // 2, KC + (j + 1) // 2)
                    act.wait_ge(s["k_ps"], j + 1)
                    for i in range(2):
                        row = slice(i * HD, (i + 1) * HD)
                        copy(kH[row, j, i, :], pK[j % 2][row, 0, :])
                    wait(act, s[f"k_out{j % 2}"], 32 * (j // 2))
                    copy(k1[0][:, j % 2, :], pK[j % 2][:, 1, :]).then_inc(s["kH"], 1)
                act.wait_ge(s["zero"], 4)
                for n in range(2 * NB):
                    high(act, 2 * KC + 2 * n, 2 * KC + 2 * n + 2)
                    act.wait_ge(s["v_ps"], n + 1)
                    b, half = divmod(n, 2)
                    for i in range(2):
                        m = copy(vH[:, b, half * NPAIR // 2:(half + 1) * NPAIR // 2, i, i * HD:(i + 1) * HD], pV[n % 2][:, :, i, :])
                    m.then_inc(s["vH"], 1)

            @block.vector
            def _(dve):
                sub = lambda out, in_, hi: nc.vector.tensor_tensor(out, in_, hi.bitcast(F32), ALU.subtract)
                for i in range(2):
                    dve.wait_ge(s["cH"], i + 1)
                    sub(cL[:, 2 * i:2 * i + 2, :, :], pC[i][:, :, :, :], cH[:, 2 * i:2 * i + 2, :, :]).then_inc(s["cL"], 1)
                low(dve, 0, KC)
                for j in range(NPAIR):
                    low(dve, KC + j // 2, KC + (j + 1) // 2)
                    dve.wait_ge(s["kH"], j + 1)
                    for i in range(2):
                        row = slice(i * HD, (i + 1) * HD)
                        sub(kL[row, j, i, :], pK[j % 2][row, 0, :], kH[row, j, i, :])
                    wait(dve, s[f"k_out{j % 2}"], 32 * (j // 2))
                    sub(k1[1][:, j % 2, :], pK[j % 2][:, 1, :], k1[0][:, j % 2, :]).then_inc(s["kL"], 1)
                dve.wait_ge(s["zero"], 4)
                for n in range(2 * NB):
                    low(dve, 2 * KC + 2 * n, 2 * KC + 2 * n + 2)
                    dve.wait_ge(s["vH"], n + 1)
                    b, half = divmod(n, 2)
                    for i in range(2):
                        at = (slice(None), b, slice(half * NPAIR // 2, (half + 1) * NPAIR // 2), i, slice(i * HD, (i + 1) * HD))
                        m = sub(vL[at], pV[n % 2][:, :, i, :], vH[at])
                    m.then_inc(s["vL"], 1)

            @block.tensor
            def _(pe):
                pe.wait_ge(s["c_in"], 16)
                for a in range(KC):
                    for b in range(NB):
                        m = nc.tensor.transpose(pC[a // 2][:, a % 2, b, :], cx[:, b, a * P:(a + 1) * P], ident[:, :])
                    if a % 2:
                        m.then_inc(s["ct"], 1)
                pe.wait_ge(s["cL"], 2)
                pe.wait_ge(low_done, KC)
                for j in range(NPAIR):
                    wait(pe, s["kL"], j - 1)
                    for a in range(KC):
                        at = (slice(None), a, slice(j * P, (j + 1) * P))
                        m = split_matmuls(nc, pK[j % 2][:, :, :], (wkH[at], wkL[at]), (cH[:, a, :, :], cL[:, a, :, :]), a == 0, a == KC - 1)
                    m.then_inc(s["k_ps"], 1)
                pe.wait_ge(low_done, 2 * KC)
                for n in range(2 * NB):
                    wait(pe, s["vL"], n - 1)
                    b, half = divmod(n, 2)
                    for a in range(KC):
                        at = (slice(None), a, slice(half * INNER // 2, (half + 1) * INNER // 2))
                        m = split_matmuls(nc, pV[n % 2][:, :, :, :].rearrange("p a i d -> p (a i d)"), (cH[:, a, b, :], cL[:, a, b, :]),
                                          (wvH[at], wvL[at]), a == 0, a == KC - 1)
                    m.then_inc(s["v_ps"], 1)

        with ExitStack() as ctx:
            sb = lambda n, s, d=F32: ctx.enter_context(nc.sbuf_tensor("b_" + n, s, d))
            ps = lambda n, s: ctx.enter_context(nc.psum_tensor("b_" + n, s, F32))
            mv, rstd, var, tmp = sb("mv", [P, TILES, 2]), *(sb(n, [P, TILES]) for n in ("rstd", "var", "tmp"))
            mu = sb("mu", [P, ROWT, KEYS], U8)
            bias = sb("bias", [P, GT, KEYS])
            xb, xn = sb("xb", [P, 2, C]), sb("xn", [P, 2, C])
            xr = sb("xr", [P, 2, C])
            xH, xL = (sb(n, [P, KC, GTOK], F32R) for n in ("xH", "xL"))
            qH, qL = (sb(n, [P, 2, GTOK], F32R) for n in ("qH", "qL"))
            S = sb("S", [P, 2, SUB, KEYS])
            nm, rs, ri = (sb(n, [P, 2, SUB]) for n in ("nm", "rs", "ri"))
            tH, tL = (sb(n, [KEYS, 2, GTOK], F32R) for n in ("tH", "tL"))
            aH, aL = (sb(n, [P, NPAIR, GTOK], F32R) for n in ("aH", "aL"))
            pQ, pS = ps("pQ", [P, GTOK]), ps("pS", [P, GT, 2, KEYS])
            pT, pO = ps("pT", [KEYS, 2, GTOK]), ps("pO", [P, GTOK])
            pY = [ps(f"pY{i}", [P, C])[:, :] for i in range(2)]
            pX = [y.rearrange("p (a c) -> p a c", c=P) for y in pY]
            s = {n: ctx.enter_context(nc.semaphore("b_" + n)) for n in
                 ("m_in own k_in x_in0 x_in1 r_in0 r_in1 bias normed xt xH xL q_ps qH qL score masked nmax exp rinv prob"
                  " tp tH tL pv aH aL wo res seen out0 out1").split()}

            def groups(eng, body):
                for b in range(NB):
                    body(b * BG, b, max(b - 1, 0), b == 0, False)
                    end = (b + 1) * BG - (b == NB - 1)
                    with eng.Fori(b * BG + 1, end) as g:
                        body(g, b, b, False, False)
                body(GROUPS - 1, NB - 1, NB - 1, False, True)

            block = ctx.enter_context(nc.Block())

            @block.sync
            def _(sp):
                sp.dma_start(mu[:, :, :], mask.rearrange("(t p) k -> p t k", p=P)).then_inc(s["m_in"], 16)

                def load(t, i):
                    sp.dma_start(xb[:, i % 2, :], x1_t[:, bass.ds(t, 1), :].rearrange("p o c -> p (o c)")).then_inc(s[f"x_in{i % 2}"], 16)

                def free(g, i):
                    sp.wait_ge(s["seen"], g * GT + i + 1)
                    sp.wait_ge(s[f"out{i % 2}"], 16 * (g * (GT // 2) + i // 2 + 1))

                def reload(g, i):
                    t = g * GT + i
                    if i >= 2:
                        free(g, i - 2)
                    sp.dma_start(xr[:, i % 2, :], x1_t[:, bass.ds(t, 1), :].rearrange("p o c -> p (o c)")).then_inc(s[f"r_in{i % 2}"], 16)

                def store(t, i):
                    sp.wait_ge(s["res"], t + 1)
                    sp.dma_start(x2_t[:, bass.ds(t, 1), :].rearrange("p o c -> p (o c)"), xr[:, i % 2, :]).then_inc(s[f"out{i % 2}"], 16)

                def outputs(g):
                    for i in range(GT):
                        reload(g, i)
                        if i:
                            store(g * GT + i - 1, i - 1)
                    store(g * GT + GT - 1, GT - 1)
                    for i in range(GT - 2, GT):
                        free(g, i)
                for i in range(GT):
                    wait(sp, s["normed"], i - 1)
                    load(i, i)

                def body(g, b, pb, first, last):
                    if b > pb:
                        sp.wait_ge(s["score"], NPAIR * g)
                        for part, dst in zip(later, (kH, kL)):
                            for i in range(2):
                                row = slice(i * HD, (i + 1) * HD)
                                sp.dma_start(dst[row, :, i, :].bitcast(F32), part[row, :, :]).then_inc(s["k_in"], 16)
                    if not first:
                        outputs(g - 1)
                    if not last:
                        for i in range(GT):
                            sp.wait_ge(s["normed"], g * GT + GT + i - 1)
                            load(g * GT + GT + i, i)
                groups(sp, body)
                outputs(GROUPS - 1)

            @block.gpsimd
            def _(pool):
                def body(g, b, pb, first, last):
                    for j in range(NPAIR):
                        n = NPAIR * g + j
                        pool.wait_ge(s["rinv"], n + 1)
                        nc.gpsimd.tensor_tensor(S[:, j % 2, :, :], S[:, j % 2, :, :],
                                                ri[:, j % 2, :].unsqueeze(2).to_broadcast([P, SUB, KEYS]), ALU.mult).then_inc(s["prob"], 1)
                groups(pool, body)

            @block.scalar
            def _(act):
                def x_high(t, i):
                    act.wait_ge(s["xt"], t + 1)
                    nc.scalar.activation(xH[:, :, i * P:(i + 1) * P], pX[i % 2], ACT.Copy).then_inc(s["xH"], 1)

                def q_high(m, j):
                    act.wait_ge(s["q_ps"], m + 1)
                    wait(act, s["score"], m - 1)
                    nc.scalar.activation(qH[:, j % 2, :], pQ[:, :], ACT.Copy, scale=SCALE).then_inc(s["qH"], 1)

                def exps(m, j, start, stop):
                    act.wait_ge(s["nmax"], m + 1)
                    for i in range(start, stop):
                        e = nc.scalar.activation(S[:, j % 2, i, :], S[:, j % 2, i, :], ACT.Exp,
                                                 bias=nm[:, j % 2, i:i + 1], accum_out=rs[:, j % 2, i:i + 1])
                    if stop == SUB:
                        e.then_inc(s["exp"], 1)

                def t_high(m):
                    act.wait_ge(s["tp"], m + 1)
                    wait(act, s["pv"], m)
                    nc.scalar.activation(tH[:, :, :], pT[:, :, :], ACT.Copy).then_inc(s["tH"], 1)

                def a_high(m, g, j):
                    act.wait_ge(s["pv"], m + 1)
                    wait(act, s["wo"], GT * g)
                    nc.scalar.activation(aH[:, j, :], pO[:, :], ACT.Copy).then_inc(s["aH"], 1)
                for i in range(GT):
                    x_high(i, i)
                q_high(0, 0)

                def body(g, b, pb, first, last):
                    for j in range(NPAIR):
                        n = NPAIR * g + j
                        if j < NPAIR - 1:
                            q_high(n + 1, j + 1)
                        if not last:
                            for i in {NPAIR - 2: (0, 1), NPAIR - 1: (2, 3)}.get(j, ()):
                                x_high(GT * g + GT + i, i)
                        if j > 1 or not first:
                            a_high(n - 2, g if j > 1 else g - 1, (j - 2) % NPAIR)
                        if j == NPAIR - 1 and not last:
                            q_high(n + 1, 0)
                        exps(n, j, 0, EARLY)
                        if j or not first:
                            t_high(n - 1)
                        exps(n, j, EARLY, SUB)
                groups(act, body)
                n = NPAIR * GROUPS
                a_high(n - 2, GROUPS - 1, NPAIR - 2)
                t_high(n - 1)
                a_high(n - 1, GROUPS - 1, NPAIR - 1)

            @block.vector
            def _(dve):
                sub = lambda out, in_, hi: nc.vector.tensor_tensor(out, in_, hi.bitcast(F32), ALU.subtract)

                def norm(g, i):
                    t = g * GT + i
                    at = bass.ds(t, 1)
                    dve.wait_ge(s[f"x_in{i % 2}"], 16 * (g * (GT // 2) + i // 2 + 1))
                    wait(dve, s["xt"], t - 1)
                    nc.vector.tensor_scalar(xn[:, i % 2, :], xb[:, i % 2, :], mv[:, at, 0], rstd[:, at],
                                            ALU.subtract, ALU.mult).then_inc(s["normed"], 1)

                def x_low(t, i):
                    dve.wait_ge(s["xH"], t + 1)
                    at = (slice(None), slice(None), slice(i * P, (i + 1) * P))
                    sub(xL[at], pX[i % 2], xH[at]).then_inc(s["xL"], 1)

                def q_low(m, j):
                    dve.wait_ge(s["qH"], m + 1)
                    nc.vector.scalar_tensor_tensor(out=qL[:, j % 2, :], in0=pQ[:, :], scalar=SCALE, in1=qH[:, j % 2, :].bitcast(F32),
                                                   op0=ALU.mult, op1=ALU.subtract).then_inc(s["qL"], 1)

                def add_mask(m, g, j):
                    dve.wait_ge(s["score"], m + 1)
                    wait(dve, s["tp"], m - 1)
                    if j == 0:
                        nc.vector.tensor_scalar(bias[:, :, :], mu[:, bass.ds((g % BG) * GT, GT), :],
                                                -1.0, FMAX, ALU.add, ALU.mult).then_inc(s["bias"], 1)
                        dve.wait_ge(s["bias"], g + 1)
                    nc.vector.tensor_tensor(S[:, j % 2, :, :].rearrange("p (t i) k -> p t i k", i=2), pS[:, :, :, :],
                                            bias[:, :, :].unsqueeze(2).to_broadcast([P, GT, 2, KEYS]),
                                            ALU.add).then_inc(s["masked"], 1)

                def maximum(m, j):
                    dve.wait_ge(s["masked"], m + 1)
                    nc.vector.tensor_reduce(nm[:, j % 2, :], S[:, j % 2, :, :], axis=AX.X, op=ALU.max, negate=True).then_inc(s["nmax"], 1)

                def inverse(m, j):
                    dve.wait_ge(s["exp"], m + 1)
                    nc.vector.reciprocal(ri[:, j % 2, :], rs[:, j % 2, :]).then_inc(s["rinv"], 1)

                def t_low(m):
                    dve.wait_ge(s["tH"], m + 1)
                    sub(tL[:, :, :], pT[:, :, :], tH[:, :, :]).then_inc(s["tL"], 1)

                def a_low(m, j):
                    dve.wait_ge(s["aH"], m + 1)
                    sub(aL[:, j, :], pO[:, :], aH[:, j, :]).then_inc(s["aL"], 1)

                def add(g, i):
                    t = g * GT + i
                    dve.wait_ge(s["wo"], t + 1)
                    dve.wait_ge(s[f"r_in{i % 2}"], 16 * (g * (GT // 2) + i // 2 + 1))
                    nc.vector.tensor_tensor(xr[:, i % 2, :], pY[i % 2], xr[:, i % 2, :], ALU.add).then_inc(s["res"], 1)

                def out_stats(g, i):
                    t = g * GT + i
                    dve.wait_ge(s["res"], t + 1)
                    nc.vector.bn_stats(out=stats[:, bass.ds(t, 1), 0, :].rearrange("p o s -> p (o s)"), in_=xr[:, i % 2, :]).then_inc(s["seen"], 1)

                def outputs(g):
                    for i in range(GT):
                        add(g, i)
                        if i:
                            out_stats(g, i - 1)
                    out_stats(g, GT - 1)
                layernorm_stats(nc, Link(dve, s["own"]), stats, KC, mv, var, tmp, rstd, mybir)
                dve.wait_ge(s["m_in"], 16)
                norm(0, 0)
                norm(0, 1)
                for i in range(GT):
                    x_low(i, i)
                    if i + 2 < GT:
                        norm(0, i + 2)
                q_low(0, 0)

                def body(g, b, pb, first, last):
                    for j in range(NPAIR):
                        n = NPAIR * g + j
                        add_mask(n, g, j)
                        if j or not first:
                            inverse(n - 1, (j - 1) % NPAIR)
                        maximum(n, j)
                        if j < NPAIR - 1:
                            q_low(n + 1, j + 1)
                        if not last:
                            for i in {NPAIR - 2: (0, 1), NPAIR - 1: (2, 3)}.get(j, ()):
                                x_low(GT * g + GT + i, i)
                        if j > 1 or not first:
                            a_low(n - 2, (j - 2) % NPAIR)
                        if j == NPAIR - 1 and not last:
                            q_low(n + 1, 0)
                        if j or not first:
                            t_low(n - 1)
                        if j == 1 and not first:
                            outputs(g - 1)
                        if not last:
                            for i in {NPAIR - 4: (0, 1), NPAIR - 2: (2, 3)}.get(j, ()):
                                norm(g + 1, i)
                groups(dve, body)
                n = NPAIR * GROUPS
                inverse(n - 1, NPAIR - 1)
                a_low(n - 2, NPAIR - 2)
                t_low(n - 1)
                a_low(n - 1, NPAIR - 1)
                outputs(GROUPS - 1)

            @block.tensor
            def _(pe):
                def x_transpose(t, i, g):
                    pe.wait_ge(s["normed"], t + 1)
                    if i < 2:
                        wait(pe, s["res"], GT * (g - 1))
                    else:
                        pe.wait_ge(s["xL"], t - 1)
                    for a in range(KC):
                        m = nc.tensor.transpose(pX[i % 2][:, a, :], xn[:, i % 2, a * P:(a + 1) * P], ident[:, :])
                    m.then_inc(s["xt"], 1)

                def query(m, j):
                    wait(pe, s["qL"], m)
                    for a in range(KC):
                        at = (slice(None), a, slice(j * P, (j + 1) * P))
                        last = split_matmuls(nc, pQ[:, :], (wqH[at], wqL[at]), (xH[:, a, :], xL[:, a, :]), a == 0, a == KC - 1)
                    last.then_inc(s["q_ps"], 1)

                def scores(m, j):
                    pe.wait_ge(s["qL"], m + 1)
                    wait(pe, s["masked"], m)
                    for t in range(GT):
                        q_at = (slice(None), j % 2, slice(t * P, (t + 1) * P))
                        last = split_matmuls(nc, pS[:, t, :, :], (qH[q_at], qL[q_at]), (kH[:, j, :, :], kL[:, j, :, :]), True, True)
                    last.then_inc(s["score"], 1)

                def p_transpose(m, j):
                    pe.wait_ge(s["prob"], m + 1)
                    wait(pe, s["tL"], m)
                    for i in range(2):
                        for t in range(GT):
                            last = nc.tensor.transpose(pT[:, i, t * P:(t + 1) * P], S[:, j % 2, 2 * t + i, :], ident[:, :])
                    last.then_inc(s["tp"], 1)

                def values(m, b, j):
                    pe.wait_ge(s["tL"], m + 1)
                    wait(pe, s["aL"], m)
                    for i in range(2):
                        last = split_matmuls(nc, pO[:, :], (vH[:, b, j, i, :], vL[:, b, j, i, :]), (tH[:, i, :], tL[:, i, :]), i == 0, i == 1)
                    last.then_inc(s["pv"], 1)

                def project(g, i):
                    t = g * GT + i
                    pe.wait_ge(s["aL"], NPAIR * g + NPAIR - 1)
                    if i >= 2:
                        pe.wait_ge(s["res"], t - 1)
                    for j in range(NPAIR):
                        if j == NPAIR - 1:
                            pe.wait_ge(s["aL"], NPAIR * g + NPAIR)
                        at = (slice(None), j, slice(i * P, (i + 1) * P))
                        last = split_matmuls(nc, pY[i % 2], (aH[at], aL[at]), (woH[:, j, :], woL[:, j, :]), j == 0, j == NPAIR - 1)
                    last.then_inc(s["wo"], 1)
                for i in range(GT):
                    x_transpose(i, i, 0)
                pe.wait_ge(s["xL"], GT)
                query(0, 0)

                def body(g, b, pb, first, last):
                    if b > pb:
                        pe.wait_ge(s["k_in"], 64 * b)
                    for j in range(NPAIR):
                        n = NPAIR * g + j
                        turn = GT * g + GT
                        scores(n, j)
                        if j < NPAIR - 1:
                            query(n + 1, j + 1)
                        elif not last:
                            x_transpose(turn + 2, 2, g + 1)
                            x_transpose(turn + 3, 3, g + 1)
                        if j > 1 or not first:
                            values(n - 2, b if j > 1 else pb, (j - 2) % NPAIR)
                        if j == NPAIR - 1 and not last:
                            pe.wait_ge(s["xL"], turn + GT)
                            query(n + 1, 0)
                        if j or not first:
                            p_transpose(n - 1, (j - 1) % NPAIR)
                        if j == 1 and not first:
                            for i in range(GT):
                                project(g - 1, i)
                        if j == NPAIR - 3 and not last:
                            x_transpose(turn, 0, g + 1)
                            x_transpose(turn + 1, 1, g + 1)
                groups(pe, body)
                n = NPAIR * GROUPS
                values(n - 2, NB - 1, NPAIR - 2)
                p_transpose(n - 1, NPAIR - 1)
                values(n - 1, NB - 1, NPAIR - 1)
                for i in range(GT):
                    project(GROUPS - 1, i)


def shared_experts(nc, ident, stats, x2, gate_w, Wg, Wu, Wd, onehot, xs, base_out, mybir, bass, ExitStack):
    F32, F32R = mybir.dt.float32, mybir.dt.float32r
    ALU, ACT, AX = mybir.AluOpType, mybir.ActivationFunctionType, mybir.AxisListType
    EXP = gate_w.shape[1]
    IC = Wg.shape[1] // P
    x2_t, xs_t, out_t = (a.rearrange("(t p) c -> p t c", p=P) for a in (x2, xs, base_out))
    with ExitStack() as ctx:
        sb = lambda n, s, d=F32: ctx.enter_context(nc.sbuf_tensor("c_" + n, s, d))
        ps = lambda n, s: ctx.enter_context(nc.psum_tensor("c_" + n, s, F32))
        wgH, wgL, wuH, wuL = (sb(n, [P, KC, IC * P], F32R) for n in ("wgH", "wgL", "wuH", "wuL"))
        wdH, wdL = (sb(n, [P, IC, C], F32R) for n in ("wdH", "wdL"))
        rw, (rH, rL) = sb("rw", [P, KC, EXP]), (sb(n, [P, KC, EXP], F32R) for n in ("rH", "rL"))
        ramp, desc = sb("ramp", [P, EXP], mybir.dt.int32), sb("desc", [P, EXP])
        mv, rstd, var, tmp = sb("mv", [P, TILES, 2]), *(sb(n, [P, TILES]) for n in ("rstd", "var", "tmp"))
        xb, x3 = sb("xb", [P, 2, C]), sb("x3", [P, GT, C])
        xr, o3, xo = sb("xr", [P, 2, C]), sb("o3", [P, 2, C]), sb("xo", [P, GT, C])
        xH, xL = (sb(n, [P, KC, GTOK], F32R) for n in ("xH", "xL"))
        sg, h = sb("sg", [P, 2, GTOK]), sb("h", [P, 2, GTOK])
        hH, hL = (sb(n, [P, IC, GTOK], F32R) for n in ("hH", "hL"))
        top, score, first_of = sb("top", [P, GT]), sb("score", [P, GT]), sb("first_of", [P, GT])
        rank = sb("rank", [P, GT, EXP])
        pG = [ps(f"pG{i}", [P, GTOK]) for i in range(2)]
        pU = [ps(f"pU{i}", [P, GTOK]) for i in range(2)]
        pD = [ps(f"pD{i}", [P, C]) for i in range(2)]
        pX, pR = ps("pX", [P, KC, P]), ps("pR", [P, GT, EXP])
        s = {n: ctx.enter_context(nc.semaphore("c_" + n)) for n in
             ("ramp g_in rH rL x_in0 x_in1 r_in0 r_in1 normed xt xH xL gate up sig gated h hH hL logit top own score xs xs_out"
              " down sum out0 out1").split()}
        SL = 16
        RL = 4
        parts = []
        for w, hi, lo in ((Wg, wgH, wgL), (Wu, wuH, wuL)):
            w_v = w.rearrange("(a p) n -> p a n", p=P)
            parts += [(w_v[:, a, :], hi[:, a, :], lo[:, a, :]) for a in range(KC)]
        wd_v = Wd.rearrange("(a p) n -> p a n", p=P)
        parts += [(wd_v[:, a:a + 2, :], wdH[:, a:a + 2, :], wdL[:, a:a + 2, :]) for a in range(0, IC, 2)]
        load_parts, high_parts, low_parts, low_done = split_weights(nc, ctx, "c_", parts, mybir)

        def groups(eng, body):
            body(0, True, False)
            with eng.Fori(1, GROUPS - 1) as g:
                body(g, False, False)
            body(GROUPS - 1, False, True)

        block = ctx.enter_context(nc.Block())
        row = lambda a, t: a[:, bass.ds(t, 1), :].rearrange("p o c -> p (o c)")

        @block.sync
        def _(sp):
            def load(t, i):
                sp.dma_start(xb[:, i % 2, :], row(x2_t, t)).then_inc(s[f"x_in{i % 2}"], 16)
            sp.dma_start(rw[:, :, :], gate_w.rearrange("(a p) n -> p a n", p=P)).then_inc(s["g_in"], 16)
            load(0, 0)
            load(1, 1)
            load_parts(sp, 0, KC)
            for i in range(2, GT):
                sp.wait_ge(s["normed"], i - 1)
                load(i, i)
            load_parts(sp, KC)

            def body(g, first, last):
                sp.wait_ge(s["xs"], g + 1)
                sp.dma_start(xs_t[:, bass.ds(g * GT, GT), :], xo[:, :, :]).then_inc(s["xs_out"], 16)
                for i in range(GT):
                    t = g * GT + i
                    if not last:
                        sp.wait_ge(s["normed"], t + GT - 1)
                        load(t + GT, i)
                    wait(sp, s["sum"], t - 1)
                    sp.dma_start(xr[:, i % 2, :], row(x2_t, t)).then_inc(s[f"r_in{i % 2}"], 16)
                    if i:
                        store(t - 1, i - 1)
                store(t, GT - 1)

            def store(t, i):
                sp.wait_ge(s["sum"], t + 1)
                sp.dma_start(row(out_t, t), o3[:, i % 2, :]).then_inc(s[f"out{i % 2}"], 16)
            groups(sp, body)
            sp.wait_ge(s["xs_out"], 16 * GROUPS)
            for i in range(2):
                sp.wait_ge(s[f"out{i}"], 16 * TILES // 2)

        @block.gpsimd
        def _(pool):
            nc.gpsimd.iota(ramp[:, :], pattern=[[-1, EXP]], base=EXP, channel_multiplier=0).then_inc(s["ramp"], 1)

        @block.scalar
        def _(act):
            def x_high(t, i):
                act.wait_ge(s["xt"], t + 1)
                nc.scalar.activation(xH[:, :, i * P:(i + 1) * P], pX[:, :, :], ACT.Copy).then_inc(s["xH"], 1)
            act.wait_ge(s["g_in"], 16)
            nc.scalar.activation(rH[:, :, :], rw[:, :, :], ACT.Copy).then_inc(s["rH"], 1)
            high_parts(act, 0, KC)
            for i in range(GT):
                x_high(i, i)
            high_parts(act, KC, 2 * KC)

            def body(g, first, last):
                for i in range(IC):
                    n = IC * g + i
                    act.wait_ge(s["gate"], n + 1)
                    wait(act, s["h"], n - 1)
                    nc.scalar.activation(sg[:, i % 2, :], pG[i % 2][:, :], ACT.Sigmoid).then_inc(s["sig"], 1)
                    if i == 1:
                        act.wait_ge(s["top"], g + 1)
                        nc.scalar.activation(score[:, :], top[:, :], ACT.Sigmoid).then_inc(s["score"], 1)
                    act.wait_ge(s["h"], n + 1)
                    if i == 0:
                        wait(act, s["down"], GT * g)
                    nc.scalar.activation(hH[:, i, :], h[:, i % 2, :], ACT.Copy).then_inc(s["hH"], 1)
                    if first:
                        high_parts(act, 2 * KC + i // 2, 2 * KC + (i + 1) // 2)
                if not last:
                    for i in range(GT):
                        x_high(GT * g + GT + i, i)
            groups(act, body)

        @block.vector
        def _(dve):
            sub = lambda out, in_, hi: nc.vector.tensor_tensor(out, in_, hi.bitcast(F32), ALU.subtract)

            def norm(g, i):
                t = g * GT + i
                at = bass.ds(t, 1)
                dve.wait_ge(s[f"x_in{i % 2}"], 16 * (g * (GT // 2) + i // 2 + 1))
                nc.vector.tensor_scalar(x3[:, i, :], xb[:, i % 2, :], mv[:, at, 0], rstd[:, at],
                                        ALU.subtract, ALU.mult).then_inc(s["normed"], 1)

            def x_low(t, i):
                dve.wait_ge(s["xH"], t + 1)
                at = (slice(None), slice(None), slice(i * P, (i + 1) * P))
                sub(xL[at], pX[:, :, :], xH[at]).then_inc(s["xL"], 1)

            def route(g):
                link = Link(dve, s["own"], SL + RL * g)
                dve.wait_ge(s["logit"], g + 1)
                wait(dve, s["score"], g)
                wide = lambda v: v.unsqueeze(2).to_broadcast([P, GT, EXP])
                nc.vector.tensor_reduce(top[:, :], pR[:, :, :], axis=AX.X, op=ALU.max).then_inc(s["top"], 1)
                dve.wait_ge(s["top"], g + 1)
                link(nc.vector.tensor_tensor(rank[:, :, :], pR[:, :, :], wide(top[:, :]), ALU.is_equal))
                link(nc.vector.tensor_tensor(rank[:, :, :], rank[:, :, :], desc[:, :].unsqueeze(1).to_broadcast([P, GT, EXP]), ALU.mult))
                link(nc.vector.tensor_reduce(first_of[:, :], rank[:, :, :], axis=AX.X, op=ALU.max))
                link(nc.vector.tensor_tensor(onehot[:, bass.ds(g * GT, GT), :], rank[:, :, :], wide(first_of[:, :]), ALU.is_equal))
                assert link.n == RL

            def scale(g):
                dve.wait_ge(s["score"], g + 1)
                if not (isinstance(g, int) and g == 0):
                    dve.wait_ge(s["xs_out"], 16 * g)
                for i in range(GT):
                    m = nc.vector.tensor_scalar(xo[:, i, :], x3[:, i, :], score[:, i:i + 1], None, ALU.mult)
                m.then_inc(s["xs"], 1)
            dve.wait_ge(s["ramp"], 1)
            nc.vector.tensor_copy(desc[:, :], ramp[:, :])
            dve.wait_ge(s["rH"], 1)
            nc.vector.tensor_tensor(rL[:, :, :], rw[:, :, :], rH[:, :, :].bitcast(F32), ALU.subtract).then_inc(s["rL"], 1)
            link = Link(dve, s["own"])
            layernorm_stats(nc, link, stats, 1, mv, var, tmp, rstd, mybir)
            assert link.n == SL
            norm(0, 0)
            norm(0, 1)
            low_parts(dve, 0, KC)
            for i in range(GT):
                x_low(i, i)
                if i + 2 < GT:
                    norm(0, i + 2)
            low_parts(dve, KC, 2 * KC)

            def body(g, first, last):
                for i in range(IC):
                    n = IC * g + i
                    dve.wait_ge(s["sig"], n + 1)
                    nc.vector.tensor_tensor(sg[:, i % 2, :], sg[:, i % 2, :], pG[i % 2][:, :], ALU.mult).then_inc(s["gated"], 1)
                    dve.wait_ge(s["gated"], n + 1)
                    dve.wait_ge(s["up"], n + 1)
                    wait(dve, s["hL"], n - 1)
                    nc.vector.tensor_tensor(h[:, i % 2, :], sg[:, i % 2, :], pU[i % 2][:, :], ALU.mult).then_inc(s["h"], 1)
                    if i == 0:
                        route(g)
                    if i == 2:
                        scale(g)
                    dve.wait_ge(s["hH"], n + 1)
                    sub(hL[:, i, :], h[:, i % 2, :], hH[:, i, :]).then_inc(s["hL"], 1)
                    if first:
                        low_parts(dve, 2 * KC + i // 2, 2 * KC + (i + 1) // 2)
                    if i == IC - 3 and not last:
                        dve.wait_ge(s["xs"], g + 1)
                        norm(g + 1, 0)
                for i in range(GT):
                    if not last:
                        x_low(GT * g + GT + i, i)
                        if i < GT - 1:
                            norm(g + 1, i + 1)
                    t = GT * g + i
                    dve.wait_ge(s["down"], t + 1)
                    dve.wait_ge(s[f"r_in{i % 2}"], 16 * (g * (GT // 2) + i // 2 + 1))
                    wait(dve, s[f"out{i % 2}"], 16 * (g * (GT // 2) + i // 2))
                    nc.vector.tensor_tensor(o3[:, i % 2, :], pD[i % 2][:, :], xr[:, i % 2, :], ALU.add).then_inc(s["sum"], 1)
            groups(dve, body)

        @block.tensor
        def _(pe):
            def x_transpose(t, i):
                pe.wait_ge(s["normed"], t + 1)
                wait(pe, s["xL"], t)
                for a in range(KC):
                    m = nc.tensor.transpose(pX[:, a, :], x3[:, i, a * P:(a + 1) * P], ident[:, :])
                m.then_inc(s["xt"], 1)
            for i in range(GT):
                x_transpose(i, i)

            def hidden(out, wH, wL, i, count):
                for a in range(KC):
                    at = (slice(None), a, slice(i * P, (i + 1) * P))
                    m = split_matmuls(nc, out, (wH[at], wL[at]), (xH[:, a, :], xL[:, a, :]), a == 0, a == KC - 1)
                m.then_inc(count, 1)

            def logits(g):
                pe.wait_ge(s["own"], SL + RL * g)
                for t in range(GT):
                    for a in range(KC):
                        at = (slice(None), a, slice(t * P, (t + 1) * P))
                        m = split_matmuls(nc, pR[:, t, :], (xH[at], xL[at]), (rH[:, a, :], rL[:, a, :]), a == 0, a == KC - 1)
                m.then_inc(s["logit"], 1)

            def body(g, first, last):
                pe.wait_ge(s["xL"], GT * g + GT)
                if first:
                    pe.wait_ge(s["rL"], 1)
                    pe.wait_ge(low_done, KC)
                for i in range(IC):
                    n = IC * g + i
                    wait(pe, s["h"], n - 1)
                    hidden(pG[i % 2][:, :], wgH, wgL, i, s["gate"])
                    if first and i == 0:
                        pe.wait_ge(low_done, 2 * KC)
                    hidden(pU[i % 2][:, :], wuH, wuL, i, s["up"])
                    if i == 0:
                        logits(g)
                for i in range(GT):
                    t = GT * g + i
                    if not last:
                        x_transpose(t + GT, i)
                    if first and i == 0:
                        pe.wait_ge(low_done, len(parts))
                    wait(pe, s["sum"], t - 1)
                    for c in range(IC):
                        if i == 0:
                            pe.wait_ge(s["hL"], IC * g + c + 1)
                        at = (slice(None), c, slice(i * P, (i + 1) * P))
                        m = split_matmuls(nc, pD[i % 2][:, :], (hH[at], hL[at]), (wdH[:, c, :], wdL[:, c, :]), c == 0, c == IC - 1)
                    m.then_inc(s["down"], 1)
            groups(pe, body)


def routing_tables(nc, onehot, index, table, weights, mybir, ExitStack):
    F32, BF, I32 = mybir.dt.float32, mybir.dt.bfloat16, mybir.dt.int32
    ALU, AX = mybir.AluOpType, mybir.AxisListType
    EXP = onehot.shape[2]
    NSLOT, NIDX = table.shape[2], index.shape[1]
    with ExitStack() as ctx:
        sb = lambda n, s, d=F32: ctx.enter_context(nc.sbuf_tensor("r_" + n, s, d))
        ps = lambda n, s: ctx.enter_context(nc.psum_tensor("r_" + n, s, F32))
        tri, ones = sb("tri", [P, P], BF), sb("ones", [P, P], BF)
        rampi, lanei = sb("rampi", [P, P], I32), sb("lanei", [P, 1], I32)
        ramp, lane, thr = sb("ramp", [P, P]), sb("lane", [P, 1]), sb("thr", [P, EXP - 1])
        A, B = sb("A", [P, TILES, EXP]), sb("B", [P, TILES, EXP])
        cmp_n, cmp_s = sb("cmp_n", [P, EXP, EXP - 1]), sb("cmp_s", [P, NSLOT + 1, EXP])
        n_e, ea, eb, st128 = sb("n_e", [P, EXP]), sb("ea", [P, EXP]), sb("eb", [P, EXP]), sb("st128", [P, EXP])
        pos, posr, posq = sb("pos", [P, TILES]), sb("posr", [P, TILES]), sb("posq", [P, TILES])
        pi, pt = sb("pi", [P, TILES], I32), sb("pt", [P, TILES], I32)
        inrow, inslot = sb("inrow", [P, TILES, P], BF), sb("inslot", [P, TILES, 3, NIDX], BF)
        e_of, act_f, idx_f = sb("e_of", [P, NSLOT + 1]), sb("act_f", [P, NSLOT]), sb("idx_f", [P, NIDX])
        pR, pT = ps("pR", [P, 2, TILES // 2, EXP]), ps("pT", [P, 2, TILES // 2, EXP])
        pI = ps("pI", [P, 3, NIDX])
        s = {n: ctx.enter_context(nc.semaphore("r_" + n)) for n in "ones tri rampi own counted placed indexed".split()}
        block = ctx.enter_context(nc.Block())

        @block.sync
        def _(sp):
            for n in range(weights.pieces):
                weights.load(sp, 0, n)

        @block.scalar
        def _(act):
            for n in range(weights.pieces):
                weights.high(act, nc.scalar.copy, 0, n)

        @block.gpsimd
        def _(pool):
            nc.gpsimd.memset(ones[:, :], 1.0).then_inc(s["ones"], 1)
            nc.gpsimd.iota(rampi[:, :], pattern=[[1, P]], base=0, channel_multiplier=0).then_inc(s["rampi"], 1)
            nc.gpsimd.iota(lanei[:, :], pattern=[[0, 1]], base=0, channel_multiplier=1).then_inc(s["rampi"], 1)
            pool.wait_ge(s["ones"], 1)
            nc.gpsimd.affine_select(out=tri[:, :], in_=ones[:, :], compare_op=ALU.is_gt, fill=0.0,
                                    base=0, pattern=[[1, P]], channel_multiplier=-1).then_inc(s["tri"], 1)
            for n in range(weights.pieces):
                weights.low(pool, nc.gpsimd, 0, n)

        @block.tensor
        def _(pe):
            pe.wait_ge(s["tri"], 1)
            half = TILES // 2
            for i in range(2):
                nc.tensor.matmul(pR[:, i, :, :], tri[:, :], onehot[:, i * half:(i + 1) * half, :], start=True, stop=True)
            for i in range(2):
                m = nc.tensor.matmul(pT[:, i, :, :], ones[:, :], onehot[:, i * half:(i + 1) * half, :], start=True, stop=True)
            m.then_inc(s["counted"], 1)
            pe.wait_ge(s["placed"], 1)
            for t in range(TILES):
                m = nc.tensor.matmul(pI[:, :, :], inrow[:, t, :], inslot[:, t, :, :], start=t == 0, stop=t == TILES - 1)
            m.then_inc(s["indexed"], 1)

        @block.vector
        def _(dve):
            v = nc.vector
            link = Link(dve, s["own"])
            flat = lambda a: a.rearrange("p i t e -> p (i t) e")
            dve.wait_ge(s["rampi"], 2)
            link(v.tensor_copy(ramp[:, :], rampi[:, :]))
            link(v.tensor_copy(lane[:, :], lanei[:, :]))
            link(v.tensor_scalar(thr[:, :], ramp[:, 1:EXP], float(P), None, ALU.mult))
            dve.wait_ge(s["counted"], 1)
            link(v.tensor_copy(A[:, :, :], flat(pT[:, :, :, :])))

            def running(a, b, n, axis_len):
                d = 1
                while d < axis_len:
                    v.tensor_copy(b[:, 0:d], a[:, 0:d])
                    link(v.tensor_tensor(b[:, d:], a[:, d:], a[:, 0:axis_len - d], ALU.add))
                    a, b, d = b, a, 2 * d
                return a
            incl = running(A, B, TILES, TILES)
            link(v.tensor_tensor(cmp_n[:, :, :], incl[:, TILES - 1, :].unsqueeze(2).to_broadcast([P, EXP, EXP - 1]),
                                 thr[:, :].unsqueeze(1).to_broadcast([P, EXP, EXP - 1]), ALU.is_gt))
            link(v.tensor_reduce(n_e[:, :], cmp_n[:, :, :], axis=AX.X, op=ALU.add))
            link(v.tensor_scalar(n_e[:, :], n_e[:, :], 1.0, None, ALU.add))
            link(v.tensor_copy(ea[:, :], n_e[:, :]))
            end = running(ea, eb, EXP, EXP)
            link(v.tensor_tensor(st128[:, :], end[:, :], n_e[:, :], ALU.subtract))
            link(v.tensor_scalar(st128[:, :], st128[:, :], float(P), None, ALU.mult))
            other = B if incl is A else A
            link(v.tensor_tensor(other[:, :, :], incl[:, :, :], flat(pT[:, :, :, :]), ALU.subtract))
            link(v.tensor_tensor(other[:, :, :], other[:, :, :], flat(pR[:, :, :, :]), ALU.add))
            link(v.tensor_tensor(other[:, :, :], other[:, :, :], st128[:, :].unsqueeze(1).to_broadcast([P, TILES, EXP]), ALU.add))
            link(v.tensor_tensor(other[:, :, :], other[:, :, :], onehot[:, :, :], ALU.mult))
            link(v.tensor_reduce(pos[:, :], other[:, :, :], axis=AX.X, op=ALU.add))
            link(v.tensor_copy(pi[:, :], pos[:, :]))
            link(v.tensor_single_scalar(pt[:, :], pi[:, :], P - 1, op=ALU.bitwise_and))
            link(v.tensor_copy(posr[:, :], pt[:, :]))
            link(v.tensor_single_scalar(pi[:, :], pi[:, :], P.bit_length() - 1, op=ALU.logical_shift_right))
            link(v.tensor_copy(posq[:, :], pi[:, :]))
            link(v.tensor_tensor(inrow[:, :, :], posr[:, :].unsqueeze(2).to_broadcast([P, TILES, P]),
                                 ramp[:, :].unsqueeze(1).to_broadcast([P, TILES, P]), ALU.is_equal))
            link(v.tensor_tensor(inslot[:, :, 0, :], posq[:, :].unsqueeze(2).to_broadcast([P, TILES, NIDX]),
                                 ramp[:, 0:NIDX].unsqueeze(1).to_broadcast([P, TILES, NIDX]), ALU.is_equal))
            link(v.tensor_scalar(inslot[:, :, 1, :], inslot[:, :, 0, :], lane[:, 0:1], None, ALU.mult))
            link(v.tensor_tensor(inslot[:, :, 2, :], inslot[:, :, 0, :], ramp[:, 0:TILES].unsqueeze(2).to_broadcast([P, TILES, NIDX]), ALU.mult))
            v.tensor_copy(idx_f[:, :], ramp[:, 0:NIDX]).then_inc(s["placed"], 1)
            link(v.tensor_tensor(cmp_s[:, :, :], ramp[:, 0:NSLOT + 1].unsqueeze(2).to_broadcast([P, NSLOT + 1, EXP]),
                                 end[:, :].unsqueeze(1).to_broadcast([P, NSLOT + 1, EXP]), ALU.is_ge))
            link(v.tensor_reduce(e_of[:, :], cmp_s[:, :, :], axis=AX.X, op=ALU.add))
            link(v.tensor_copy(table[:, 1, :], e_of[0:1, 0:NSLOT]))
            link(v.tensor_copy(table[:, 2, :], end[0:1, EXP - 1:EXP].to_broadcast([1, NSLOT])))
            link(v.tensor_tensor(act_f[:, :], e_of[:, 1:NSLOT + 1], e_of[:, 0:NSLOT], ALU.subtract))
            link(v.scalar_tensor_tensor(out=act_f[:, :], in0=e_of[:, 0:NSLOT], scalar=float(EXP - 1), in1=act_f[:, :],
                                        op0=ALU.is_lt, op1=ALU.mult))
            link(v.scalar_tensor_tensor(out=act_f[:, :], in0=e_of[:, 0:NSLOT], scalar=float(EXP), in1=act_f[:, :],
                                        op0=ALU.is_lt, op1=ALU.add))
            link(v.tensor_copy(table[:, 0, :], act_f[0:1, :]))
            dve.wait_ge(s["indexed"], 1)
            link(v.tensor_scalar(idx_f[:, :], pI[:, 0, :], -float(TOK), float(TOK), ALU.mult, ALU.add))
            link(v.tensor_tensor(idx_f[:, :], idx_f[:, :], pI[:, 1, :], ALU.add))
            link(v.scalar_tensor_tensor(out=idx_f[:, :], in0=pI[:, 2, :], scalar=float(P), in1=idx_f[:, :], op0=ALU.mult, op1=ALU.add))
            link(v.tensor_copy(index[:, :], idx_f[:, :]))


class ExpertWeights:

    def __init__(self, nc, ctx, Wg, Wu, Wd, mybir, bass):
        F32, F32R = mybir.dt.float32, mybir.dt.float32r
        self.nc, self.Wg, self.Wu, self.Wd, self.bass, self.F32, self.sub = nc, Wg, Wu, Wd, bass, F32, mybir.AluOpType.subtract
        self.half = Wg.shape[2] // 2
        self.gate_up = 2 * KC
        self.pieces = self.gate_up + Wg.shape[2] // P // 2
        self.pool_low = (1, 4, 6, 8)
        self.dve_high = (2, 8)
        sb = lambda n, d: ctx.enter_context(nc.sbuf_tensor("e_" + n, [P, self.pieces, 2, self.half], d))
        self.raw, self.wH, self.wL = sb("raw", F32), sb("wH", F32R), sb("wL", F32R)
        self.s = {n: ctx.enter_context(nc.semaphore("e_" + n)) for n in "highA highD lowD lowP".split()}
        self.arrived = [ctx.enter_context(nc.semaphore(f"e_w_in{n}")) for n in range(self.pieces)]

    def _count(self, members, complement, e, n):
        group = [m for m in range(self.pieces) if (m in members) != complement]
        return len(group) * e + sum(1 for m in group if m <= n)

    def high_count(self, n):
        return self.s["highD" if n in self.dve_high else "highA"]

    def low_count(self, n):
        return self.s["lowP" if n in self.pool_low else "lowD"]

    def wait_high(self, eng, e, n):
        eng.wait_ge(self.high_count(n), self._count(self.dve_high, n not in self.dve_high, e, n))

    def wait_low(self, eng, e, n):
        eng.wait_ge(self.low_count(n), self._count(self.pool_low, n not in self.pool_low, e, n))

    def wait_raw(self, eng, e, n):
        eng.wait_ge(self.arrived[n], (32 if n < self.gate_up else 16) * (e + 1))

    def load(self, sp, e, n):
        one = lambda w: w[self.bass.ds(e, 1), :, :].rearrange("o (a p) n -> (o a) p n", p=P)
        if n < self.gate_up:
            a, columns = n % KC, slice(n // KC * self.half, (n // KC + 1) * self.half)
            for i, w in enumerate((self.Wg, self.Wu)):
                sp.dma_start(self.raw[:, n, i, :], one(w)[a, :, columns]).then_inc(self.arrived[n], 16)
        else:
            a = 2 * (n - self.gate_up)
            sp.dma_start(self.raw[:, n, :, :], one(self.Wd)[a:a + 2, :, :].rearrange("a p n -> p a n")).then_inc(self.arrived[n], 16)

    def high(self, eng, copy, e, n):
        self.wait_raw(eng, e, n)
        copy(self.wH[:, n, :, :], self.raw[:, n, :, :]).then_inc(self.high_count(n), 1)

    def low(self, eng, unit, e, n):
        self.wait_raw(eng, e, n)
        self.wait_high(eng, e, n)
        unit.tensor_tensor(self.wL[:, n, :, :], self.raw[:, n, :, :], self.wH[:, n, :, :].bitcast(self.F32),
                           self.sub).then_inc(self.low_count(n), 1)


def routed_experts(nc, ident, xs, base, weights, index, table, out, mybir, bass, ExitStack):
    F32, F32R, I32 = mybir.dt.float32, mybir.dt.float32r, mybir.dt.int32
    ALU, ACT = mybir.AluOpType, mybir.ActivationFunctionType
    EXP, _, IW = weights.Wg.shape
    IC = IW // P
    HALF = weights.half
    BLOCK = 8
    GU, PIECES = weights.gate_up, weights.pieces
    DN = PIECES - GU
    POOL_LOW, DVE_HIGH = weights.pool_low, weights.dve_high
    DVE_LOW = tuple(n for n in range(PIECES) if n not in POOL_LOW)
    ACT_HIGH = tuple(n for n in range(PIECES) if n not in DVE_HIGH)
    wH, wL, wait_low = weights.wH, weights.wL, weights.wait_low
    with ExitStack() as ctx:
        sb = lambda n, s, d=F32: ctx.enter_context(nc.sbuf_tensor("d_" + n, s, d))
        ps = lambda n, s: ctx.enter_context(nc.psum_tensor("d_" + n, s, F32))
        xg, bg, og = sb("xg", [P, C]), sb("bg", [P, C]), sb("og", [P, C])
        ix, ib, iw = (sb(n, [P, 1], I32) for n in ("ix", "ib", "iw"))
        xH, xL = (sb(n, [P, KC, P], F32R) for n in ("xH", "xL"))
        sg, h = sb("sg", [P, 2, HALF]), sb("h", [P, 2, HALF])
        hH, hL = (sb(n, [P, IC, P], F32R) for n in ("hH", "hL"))
        pG = [ps(f"pG{i}", [P, HALF]) for i in range(2)]
        pU = [ps(f"pU{i}", [P, HALF]) for i in range(2)]
        pT = [ps(f"pT{i}", [P, IC // 2, P]) for i in range(2)]
        pX, pD = ps("pX", [P, KC, P]), ps("pD", [P, C])
        names = ("zero ix ib iw x_in b_in turn xt xH xL silu h ht hH hL used sum").split()
        s = {n: ctx.enter_context(nc.semaphore("d_" + n)) for n in names}

        def slots(eng, body):
            look = lambda i, t, top: eng.value_load(table[0:1, i, bass.ds(t, 1)], min_val=0, max_val=top)
            with eng.Fori(0, table.shape[2] // BLOCK) as b:
                with eng.If(look(0, b * BLOCK, 2) > 0):
                    with eng.Fori(0, BLOCK) as i:
                        t = b * BLOCK + i
                        kind = look(0, t, 2)
                        with eng.If(kind == 1):
                            body(t, look(1, t, EXP), False)
                        with eng.If(kind == 2):
                            body(t, look(1, t, EXP), True)

        block = ctx.enter_context(nc.Block())

        @block.sync
        def _(sp):
            with sp.Fori(1, EXP) as e:
                for n in range(PIECES):
                    wait_low(sp, e - 1, n)
                    weights.load(sp, e, n)

        @block.gpsimd
        def _(pool):
            indirect = bass.IndirectOffsetOnAxis
            bound = pool.to_reg(TOK - 1)
            for a in (xg, bg):
                nc.gpsimd.memset(a[:, :], 0.0).then_inc(s["zero"], 1)
            pool.wait_ge(s["zero"], 2)

            def indirect_dma(count, **how):
                pool.indirect_dma_start(bounds_check=bound, oob_is_err=False, **how).then_inc(count, 16)

            def gather_x(t, copied, count, arrived):
                nc.gpsimd.tensor_copy(ix[:, :], index[:, bass.ds(t, 1)]).then_inc(copied, 1)
                pool.wait_ge(s["zero"], 2)
                pool.wait_ge(copied, count)
                indirect_dma(arrived, out=xg[:, :], out_offset=None, in_=xs, in_offset=indirect(ap=ix[:, 0:1], axis=0))



            def gather_base(t):
                nc.gpsimd.tensor_copy(ib[:, :], index[:, bass.ds(t, 1)]).then_inc(s["ib"], 1)
                pool.wait_ge(s["zero"], 2)
                pool.wait_ge(s["ib"], t + 1)
                indirect_dma(s["b_in"], out=bg[:, :], out_offset=None, in_=base, in_offset=indirect(ap=ib[:, 0:1], axis=0))
            nc.gpsimd.memset(iw[:, :], 0).then_inc(s["iw"], 1)
            pool.wait_ge(s["iw"], 1)
            gather_x(0, s["zero"], 3, s["turn"])
            gather_base(0)
            pool.wait_ge(s["turn"], 16)
            pool.wait_ge(s["xt"], 1)
            gather_x(1, s["ix"], 1, s["x_in"])

            def body(t, e, split):
                for n in POOL_LOW:
                    if split:
                        pool.wait_ge(s["used"], PIECES * t + n + 1)
                        weights.low(pool, nc.gpsimd, e + 1, n)
                    if n == KC + 2:
                        pool.wait_ge(s["x_in"], 16 * t + 16)
                        pool.wait_ge(s["xt"], t + 2)
                        gather_x(t + 2, s["ix"], t + 2, s["x_in"])
                pool.wait_ge(s["turn"], 16 * t + 16)
                nc.gpsimd.tensor_copy(iw[:, :], index[:, bass.ds(t, 1)]).then_inc(s["iw"], 1)
                pool.wait_ge(s["zero"], 2)
                pool.wait_ge(s["iw"], t + 2)
                pool.wait_ge(s["sum"], t + 2)
                indirect_dma(s["turn"], out=out, out_offset=indirect(ap=iw[:, 0:1], axis=0), in_=og[:, :], in_offset=None)
                pool.wait_ge(s["b_in"], 16 * t + 16)
                gather_base(t + 1)
            slots(pool, body)
            used = pool.value_load(table[0:1, 2, 0:1], min_val=EXP, max_val=table.shape[2] - 1)
            pool.wait_ge(s["turn"], 16 * used + 16)
            pool.wait_ge(s["b_in"], 16 * used + 16)
            pool.wait_ge(s["x_in"], 16 * used + 16)

        @block.scalar
        def _(act):
            def x_high(t):
                act.wait_ge(s["xt"], t + 1)
                nc.scalar.copy(xH[:, :, :], pX[:, :, :]).then_inc(s["xH"], 1)
            x_high(0)

            def body(t, e, split):
                def high(*pieces):
                    for n in pieces:
                        if split and n in ACT_HIGH:
                            act.wait_ge(s["used"], PIECES * t + n + 1)
                            weights.high(act, nc.scalar.copy, e + 1, n)

                def silu(n):
                    act.wait_ge(s["used"], PIECES * t + KC * (n + 1))
                    nc.scalar.activation(sg[:, n, :], pG[n][:, :], ACT.Silu).then_inc(s["silu"], 1)

                def h_high(n):
                    act.wait_ge(s["ht"], 2 * t + n + 1)
                    nc.scalar.copy(hH[:, 4 * n:4 * n + 4, :], pT[n][:, :, :]).then_inc(s["hH"], 1)
                high(0, 1, 2)
                silu(0)
                high(3, 4)
                h_high(0)
                high(5, 6)
                silu(1)
                x_high(t + 1)
                h_high(1)
                high(7, 8, 9, 10, 11)
            slots(act, body)

        @block.vector
        def _(dve):
            sub = lambda out, in_, hi: nc.vector.tensor_tensor(out, in_, hi.bitcast(F32), ALU.subtract)

            def x_low(t):
                dve.wait_ge(s["xH"], t + 1)
                sub(xL[:, :, :], pX[:, :, :], xH[:, :, :]).then_inc(s["xL"], 1)
            x_low(0)
            for n in range(2):
                nc.vector.memset(h[:, n, :], 0.0).then_inc(s["h"], 1)
            nc.vector.memset(og[:, :], 0.0).then_inc(s["sum"], 1)

            def body(t, e, split):
                def low(*pieces):
                    for n in pieces:
                        if split:
                            if n in DVE_HIGH or n in DVE_LOW:
                                dve.wait_ge(s["used"], PIECES * t + n + 1)
                            if n in DVE_HIGH:
                                weights.high(dve, nc.vector.tensor_copy, e + 1, n)
                            if n in DVE_LOW:
                                weights.low(dve, nc.vector, e + 1, n)

                def gate(n):
                    dve.wait_ge(s["silu"], 2 * t + n + 1)
                    dve.wait_ge(s["h"], 2 * t + 2)
                    nc.vector.tensor_tensor(h[:, n, :], sg[:, n, :], pU[n][:, :], ALU.mult).then_inc(s["h"], 1)

                def h_low(n):
                    dve.wait_ge(s["hH"], 2 * t + n + 1)
                    sub(hL[:, 4 * n:4 * n + 4, :], pT[n][:, :, :], hH[:, 4 * n:4 * n + 4, :]).then_inc(s["hL"], 1)
                low(0, 1, 2)
                gate(0)
                low(3, 4)
                h_low(0)
                low(5, 6)
                gate(1)
                x_low(t + 1)
                h_low(1)
                low(7, 8, 9, 10, 11)
                dve.wait_ge(s["used"], PIECES * (t + 1))
                dve.wait_ge(s["b_in"], 16 * t + 16)
                dve.wait_ge(s["turn"], 16 * t + 16)
                dve.wait_ge(s["sum"], t + 1)
                nc.vector.tensor_tensor(og[:, :], pD[:, :], bg[:, :], ALU.add).then_inc(s["sum"], 1)
            slots(dve, body)

        @block.tensor
        def _(pe):
            def x_transpose(arrived, count):
                pe.wait_ge(arrived, count)
                for a in range(KC):
                    m = nc.tensor.transpose(pX[:, a, :], xg[:, a * P:(a + 1) * P], ident[:, :])
                m.then_inc(s["xt"], 1)
            x_transpose(s["turn"], 16)

            def body(t, e, split):
                def gate_up(half, chunks):
                    for a in chunks:
                        n = half * KC + a
                        wait_low(pe, e, n)
                        for i, (x, w, first, last) in enumerate(((xH, wH, a == 0, False), (xH, wL, False, False), (xL, wH, False, a == KC - 1))):
                            for j, bank in enumerate((pG, pU)):
                                m = nc.tensor.matmul(bank[half][:, :], x[:, a, :], w[:, n, j, :], start=first, stop=last)
                        m.then_inc(s["used"], 1)

                def h_transpose(half):
                    pe.wait_ge(s["h"], 2 * t + 2 + half + 1)
                    for c in range(IC // 2):
                        m = nc.tensor.transpose(pT[half][:, c, :], h[:, half, c * P:(c + 1) * P], ident[:, :])
                    m.then_inc(s["ht"], 1)

                def down(n):
                    wait_low(pe, e, n)
                    pe.wait_ge(s["hL"], 2 * t + (n - GU) // (DN // 2) + 1)
                    for i in range(2):
                        c = 2 * (n - GU) + i
                        m = split_matmuls(nc, pD[:, :], (hH[:, c, :], hL[:, c, :]), (wH[:, n, i, :], wL[:, n, i, :]), c == 0, c == IC - 1)
                    return m.then_inc(s["used"], 1)
                pe.wait_ge(s["xL"], t + 1)
                pe.wait_ge(s["h"], 2 * t + 2)
                gate_up(0, range(KC))
                gate_up(1, range(KC // 2))
                h_transpose(0)
                gate_up(1, range(KC // 2, KC))
                x_transpose(s["x_in"], 16 * t + 16)
                pe.wait_ge(s["sum"], t + 1)
                down(GU)
                h_transpose(1)
                for n in range(GU + 1, PIECES):
                    down(n)
            slots(pe, body)


def decoder_layer(nc, x, ctx_in, mask, w_fc, w_proj, ln_g, ln_b, Wq, Wk, Wv, Wo, gate_w, sg_w, su_w, sd_w, rg_w, ru_w, rd_w, out):
    F32 = mybir.dt.float32
    x1, x2, xs, base = (nc.dram_tensor(n, (TOK, C), F32, kind="Internal").ap() for n in ("x1", "x2", "xs", "base"))
    slots = 2 * (TOK // P)
    experts = gate_w.shape[1]
    with ExitStack() as ctx:
        ident = ctx.enter_context(nc.sbuf_tensor("ident", [P, P], F32))
        stats = ctx.enter_context(nc.sbuf_tensor("stats", [P, TILES, KC, 6], F32))
        self_attention(nc, ident, stats, x, w_fc, w_proj, ln_g, ln_b, x1, mybir, bass, ExitStack)
        cross_attention(nc, ident, stats, x1, ctx_in, mask, Wq, Wk, Wv, Wo, x2, mybir, bass, ExitStack)
        onehot = ctx.enter_context(nc.sbuf_tensor("onehot", [P, TILES, experts], mybir.dt.bfloat16))
        index = ctx.enter_context(nc.sbuf_tensor("index", [P, slots + 2], mybir.dt.int32))
        table = ctx.enter_context(nc.sbuf_tensor("table", [1, 3, slots], mybir.dt.int32))
        shared_experts(nc, ident, stats, x2, gate_w, sg_w, su_w, sd_w, onehot, xs, base, mybir, bass, ExitStack)
        weights = ExpertWeights(nc, ctx, rg_w, ru_w, rd_w, mybir, bass)
        routing_tables(nc, onehot, index, table, weights, mybir, ExitStack)
        routed_experts(nc, ident, xs, base, weights, index, table, out, mybir, bass, ExitStack)


_INS = ["x", "ctx_1024", "mask_SxS2_bk0", "L0_attn_w_fc", "L0_attn_w_proj", "L0_attn_ln_g", "L0_attn_ln_b",
        "L0_xattn_Wq", "L0_xattn_Wk", "L0_xattn_Wv", "L0_xattn_Wo", "L0_ffn_gate_w", "L0_ffn_shared_gate_w",
        "L0_ffn_shared_up_w", "L0_ffn_shared_down_w", "L0_ffn_routed_gate_w", "L0_ffn_routed_up_w", "L0_ffn_routed_down_w"]


def kernel(**inputs):
    import numpy as np
    import concourse.bacc as bacc
    from concourse.bass_utils import run_bass_kernel_spmd

    nc = bacc.Bacc("TRN2", target_bir_lowering=False, num_devices=1)
    arrays, args = {}, []
    for name in _INS:
        a = np.ascontiguousarray(inputs[name])
        if name == "x":
            a = a.reshape(TOK, C)
        arrays[f"in_{name}"] = a
        args.append(nc.dram_tensor(f"in_{name}", a.shape, mybir.dt.from_np(a.dtype), kind="ExternalInput").ap())
    out = nc.dram_tensor("out_0", (TOK, C), mybir.dt.float32, kind="ExternalOutput").ap()
    decoder_layer(nc, *args, out)
    r = run_bass_kernel_spmd(nc, [arrays], core_ids=[0])
    return r.results[0]["out_0"].reshape(NB, TOK // NB, C)
```
